# Optimizing a Trainium2 kernel written in Bass

```python
import numpy as np
import jax
import jax.numpy as jnp

def _softmax(x, axis=-1):
    return jax.nn.softmax(x, axis=axis)

def _gelu(x):
    return jax.nn.gelu(x, approximate=True)

def _silu(x):
    return jax.nn.silu(x)

def _sigmoid(x):
    return jax.nn.sigmoid(x)

def _layernorm(x, axis=-1, eps=1e-05):
    m = jnp.mean(x, axis=axis, keepdims=True)
    v = jnp.var(x, axis=axis, keepdims=True)
    return (x - m) / jnp.sqrt(v + eps)

def _scatter_add(tgt, idx, src, axis=0):
    return tgt.at[idx].add(src)

def _segment_sum(src, seg, n):
    return jax.ops.segment_sum(src, seg, n)
kernel_name = 'mk_gnn_resnorm_d2_gnn_r32_0ab05b'

def setup_inputs(seed: int=0):
    np.random.seed(seed)
    _w = jnp.asarray

    def _rec_inputs():
        import jax
        import jax.numpy as jnp
        _gk = jax.random.key(seed)
        x = -0.000202 + 1 * jax.random.normal(jax.random.fold_in(_gk, 1), (50000, 128), jnp.float32)
        src = jax.random.randint(jax.random.fold_in(_gk, 2), (50000,), 0, 50000, jnp.int32)
        dst = jnp.minimum((50000 * jax.random.uniform(jax.random.fold_in(_gk, 3), (50000,)) ** 2.0).astype(jnp.int32), 49999)
        _o = jnp.argsort(dst, stable=True)
        src = src[_o]
        dst = dst[_o]
        return (x, src, dst)
    x, src, dst = _rec_inputs()

    def _L0_gnn_setup():
        import jax, jax.numpy as jnp
        import numpy as np
        N_NODES = 50000
        N_EDGES = 18750
        D_IN = 128
        D_OUT = 128
        BN_EPS = 1e-05
        key = jax.random.key(seed)
        ks = jax.random.split(key, 6)
        X = jax.random.normal(ks[0], (N_NODES, D_IN), dtype=jnp.float32)
        W = jax.random.normal(ks[1], (D_IN, D_OUT), dtype=jnp.float32) * (1.0 / np.sqrt(D_IN))
        Wres = jax.random.normal(ks[2], (D_IN, D_OUT), dtype=jnp.float32) * (1.0 / np.sqrt(D_IN))
        gamma = jnp.ones((D_OUT,), dtype=jnp.float32)
        beta = jnp.zeros((D_OUT,), dtype=jnp.float32)
        src = jax.random.randint(ks[3], (N_EDGES,), 0, N_NODES, dtype=jnp.int32)
        dst = jax.random.randint(ks[4], (N_EDGES,), 0, N_NODES, dtype=jnp.int32)
        return {'X': X, 'W': W, 'Wres': Wres, 'gamma': gamma, 'beta': beta, 'src': src, 'dst': dst}
    _L0_gnn_all = _L0_gnn_setup()
    _L0_gnn_in = {k: v for k, v in _L0_gnn_all.items() if k in ('W', 'Wres', 'gamma', 'beta')}
    del _L0_gnn_all

    def _L1_gnn_setup():
        import jax, jax.numpy as jnp
        import numpy as np
        N = 50000
        E = 25000
        D = 128
        L = 2
        EPS = 1e-05

        def _layer_norm(y, g, b):
            mu = jnp.mean(y, axis=-1, keepdims=True)
            var = jnp.mean((y - mu) ** 2, axis=-1, keepdims=True)
            return (y - mu) * jax.lax.rsqrt(var + EPS) * g + b
        key = jax.random.key(seed)
        ks = jax.random.split(key, 16)
        x = jax.random.normal(ks[0], (N, D), dtype=jnp.float32)
        edge_index = jax.random.randint(ks[1], (2, E), 0, N, dtype=jnp.int64)
        s = 1.0 / np.sqrt(D)
        s2 = 1.0 / np.sqrt(2 * D)
        return {'x': x, 'edge_index': edge_index, 'W_enc': jax.random.normal(ks[2], (D, D), jnp.float32) * s, 'b_enc': jnp.zeros((D,), jnp.float32), 'msg_W1': jax.random.normal(ks[3], (L, D, 2 * D), jnp.float32) * s2, 'msg_b1': jnp.zeros((L, D), jnp.float32), 'msg_W2': jax.random.normal(ks[4], (L, D, D), jnp.float32) * s, 'msg_b2': jnp.zeros((L, D), jnp.float32), 'upd_W': jax.random.normal(ks[5], (L, D, 2 * D), jnp.float32) * s2, 'upd_b': jnp.zeros((L, D), jnp.float32), 'ln_g': jnp.ones((L, D), jnp.float32), 'ln_b': jnp.zeros((L, D), jnp.float32), 'W_out': jax.random.normal(ks[6], (D, D), jnp.float32) * s, 'b_out': jnp.zeros((D,), jnp.float32)}
    _L1_gnn_all = _L1_gnn_setup()
    _L1_gnn_in = {k: v for k, v in _L1_gnn_all.items() if k in ('W_enc', 'b_enc', 'msg_W1', 'msg_b1', 'msg_W2', 'msg_b2', 'upd_W', 'upd_b', 'ln_g', 'ln_b', 'W_out', 'b_out')}
    del _L1_gnn_all
    return {'x': x, 'src': src, 'dst': dst, 'L0_gnn_W': _L0_gnn_in['W'], 'L0_gnn_Wres': _L0_gnn_in['Wres'], 'L0_gnn_gamma': _L0_gnn_in['gamma'], 'L0_gnn_beta': _L0_gnn_in['beta'], 'L1_gnn_W_enc': _L1_gnn_in['W_enc'], 'L1_gnn_b_enc': _L1_gnn_in['b_enc'], 'L1_gnn_msg_W1': _L1_gnn_in['msg_W1'], 'L1_gnn_msg_b1': _L1_gnn_in['msg_b1'], 'L1_gnn_msg_W2': _L1_gnn_in['msg_W2'], 'L1_gnn_msg_b2': _L1_gnn_in['msg_b2'], 'L1_gnn_upd_W': _L1_gnn_in['upd_W'], 'L1_gnn_upd_b': _L1_gnn_in['upd_b'], 'L1_gnn_ln_g': _L1_gnn_in['ln_g'], 'L1_gnn_ln_b': _L1_gnn_in['ln_b'], 'L1_gnn_W_out': _L1_gnn_in['W_out'], 'L1_gnn_b_out': _L1_gnn_in['b_out']}

def reference(x, src, dst, L0_gnn_W, L0_gnn_Wres, L0_gnn_gamma, L0_gnn_beta, L1_gnn_W_enc, L1_gnn_b_enc, L1_gnn_msg_W1, L1_gnn_msg_b1, L1_gnn_msg_W2, L1_gnn_msg_b2, L1_gnn_upd_W, L1_gnn_upd_b, L1_gnn_ln_g, L1_gnn_ln_b, L1_gnn_W_out, L1_gnn_b_out):
    import jax
    import jax.numpy as jnp

    def _L0_gnn_ref(X, W, Wres, gamma, beta, src, dst):
        import jax, jax.numpy as jnp
        import numpy as np
        N_NODES = 50000
        N_EDGES = 18750
        D_IN = 128
        D_OUT = 128
        BN_EPS = 1e-05
        N = X.shape[0]
        ones_e = jnp.ones(src.shape[0], dtype=X.dtype)
        deg_out = jnp.clip(jax.ops.segment_sum(ones_e, src, num_segments=N), 1.0)
        deg_in = jnp.clip(jax.ops.segment_sum(ones_e, dst, num_segments=N), 1.0)
        norm_src = jax.lax.rsqrt(deg_out)[:, None]
        norm_dst = jax.lax.rsqrt(deg_in)[:, None]
        h = X * norm_src
        agg = jax.ops.segment_sum(h[src], dst, num_segments=N)
        agg = agg * norm_dst
        gX = jax.nn.relu(agg @ W)
        gX = gX + jax.nn.relu(X @ Wres)
        mean = jnp.mean(gX, axis=0)
        var = jnp.mean(jnp.square(gX - mean), axis=0)
        out = gamma * (gX - mean) * jax.lax.rsqrt(var + BN_EPS) + beta
        return out

    def _L1_gnn_ref(x, edge_index, W_enc, b_enc, msg_W1, msg_b1, msg_W2, msg_b2, upd_W, upd_b, ln_g, ln_b, W_out, b_out):
        import jax, jax.numpy as jnp
        import numpy as np
        N = 50000
        E = 25000
        D = 128
        L = 2
        EPS = 1e-05

        def _layer_norm(y, g, b):
            mu = jnp.mean(y, axis=-1, keepdims=True)
            var = jnp.mean((y - mu) ** 2, axis=-1, keepdims=True)
            return (y - mu) * jax.lax.rsqrt(var + EPS) * g + b
        h = x @ W_enc.T + b_enc
        row, col = (edge_index[0], edge_index[1])
        n_layers = msg_W1.shape[0]
        for l in range(n_layers):
            m = jnp.concatenate([h[row], h[col]], axis=-1)
            m = jax.nn.relu(m @ msg_W1[l].T + msg_b1[l])
            m = m @ msg_W2[l].T + msg_b2[l]
            agg = jax.ops.segment_sum(m, col, num_segments=h.shape[0])
            upd = jnp.concatenate([h, agg], axis=-1) @ upd_W[l].T + upd_b[l]
            h = _layer_norm(h + upd, ln_g[l], ln_b[l])
        return h @ W_out.T + b_out
    edge_index = jnp.stack([src, dst])
    x = _layernorm(x + _L0_gnn_ref(x, L0_gnn_W, L0_gnn_Wres, L0_gnn_gamma, L0_gnn_beta, src, dst), axis=-1)
    x = _layernorm(x + _L1_gnn_ref(x, edge_index, L1_gnn_W_enc, L1_gnn_b_enc, L1_gnn_msg_W1, L1_gnn_msg_b1, L1_gnn_msg_W2, L1_gnn_msg_b2, L1_gnn_upd_W, L1_gnn_upd_b, L1_gnn_ln_g, L1_gnn_ln_b, L1_gnn_W_out, L1_gnn_b_out), axis=-1)
    return x

_drawn_inputs = setup_inputs


def setup_inputs(seed=0):
    import zlib

    import numpy as np

    out = dict(_drawn_inputs(seed))
    spreads = {'L0_gnn_gamma': (1.0, 0.2),
     'L0_gnn_beta': (0.0, 0.1),
     'L1_gnn_b_enc': (0.0, 0.1),
     'L1_gnn_msg_b1': (0.0, 0.1),
     'L1_gnn_msg_b2': (0.0, 0.1),
     'L1_gnn_upd_b': (0.0, 0.1),
     'L1_gnn_ln_g': (1.0, 0.2),
     'L1_gnn_ln_b': (0.0, 0.1),
     'L1_gnn_b_out': (0.0, 0.1)}
    factors = {}
    for name, (base, spread) in spreads.items():
        noise = np.random.default_rng([zlib.crc32(name.encode()), seed]).standard_normal(out[name].shape)
        drawn = base * np.exp(spread * noise) if base else spread * noise
        out[name] = jnp.asarray(drawn.astype(out[name].dtype))
    for name, factor in factors.items():
        out[name] = (out[name] * factor).astype(out[name].dtype)
    return out
```

```python
from contextlib import ExitStack

import concourse.bass as bass
from concourse import mybir

F32, F16, I32 = mybir.dt.float32, mybir.dt.float16, mybir.dt.int32
ALU, ACT, AX = mybir.AluOpType, mybir.ActivationFunctionType, mybir.AxisListType

P = 128
N, E, D, L = 50000, 50000, 128, 2
J = 4
CH = P * J
NC = -(-N // CH)
NPAD = NC * CH
LAST = (N - (NC - 1) * CH) // J
COLS = NC * J
TP = 392
EFULL = E // TP
EREST = E - EFULL * TP
G = 4
NG = TP // G
TRASH = NPAD
AGG = NPAD + P
EPS = 1e-5


class Mem:

    def semaphore(self, nc, name):
        self.sems.append(nc.alloc_semaphore(self.tag + name))
        return self.sems[-1]


def chunk(table, c):
    return table[bass.ds(c * CH, CH), :].rearrange("(p j) d -> p (j d)", j=J)


def chunk_rows(table, c):
    if is_last(c):
        return table[c * CH:N, :].rearrange("(p j) d -> p (j d)", j=J)
    return chunk(table, c)


def each_chunk(eng, ring, body):
    turns = (NC - 1) // ring
    for b in range(ring):
        body(b, b, 0)
    with eng.Fori(1, turns) as i:
        for b in range(ring):
            body(i * ring + b, b, i)
    for c in range(turns * ring, NC):
        body(c, c % ring, c // ring)


def each_group(eng, body):
    turns = NG // 2
    for h in range(2):
        body(h, h, 0)
    with eng.Fori(1, turns - 1) as i:
        for h in range(2):
            body(i * 2 + h, h, i)
    for h in range(2):
        body(NG - 2 + h, h, turns - 1)


def is_first(turn):
    return isinstance(turn, int) and turn == 0


def is_last(c):
    return isinstance(c, int) and c == NC - 1


def parts(c):
    return LAST if is_last(c) else P


def slot_uses(ring, b):
    return len(range(b, NC, ring))


def setup_stage(nc, m, a):
    with ExitStack() as ctx:
        sem = lambda n: m.semaphore(nc, n)
        sb = lambda n, s, d: ctx.enter_context(nc.sbuf_tensor(m.tag + n, s, d))
        pb = lambda n, s, d: ctx.enter_context(nc.psum_tensor(m.tag + n, s, d))
        iota_f = sb("iota_f", [P, COLS], F32)
        iota_h = sb("iota_h", [P, COLS], F16)
        ints = sb("ints", [P, 4, TP], I32)
        bins = sb("bins", [P, 4, TP], F32)
        low = sb("low", [P, 2, 8, P], F16)
        high = sb("high", [P, 2, 8, COLS], F16)
        zero_h = sb("zero_h", [P, COLS], F16)
        zeros = sb("zeros", [P, 2048], F32)
        ps_hist = pb("ps_hist", [P, 2, 512], F32)
        s_pad, s_edges, s_iota, s_const = sem("s_pad"), sem("s_edges"), sem("s_iota"), sem("s_const")
        s_zero, s_zeroed = sem("s_zero"), sem("s_zeroed")
        s_chain, s_hot, s_counted, s_root = sem("s_chain"), sem("s_hot"), sem("s_counted"), sem("s_root")
        with nc.Block() as block:

            @block.sync
            def _(sp):
                sp.wait_ge(s_pad, 1)
                for k, v in enumerate((a["src"], a["dst"])):
                    sp.dma_start(m.edge[0:EFULL, k, :], v[0:EFULL * TP].rearrange("(p t) -> p t", t=TP)).then_inc(s_edges, 16)
                    sp.dma_start(m.edge[EFULL:P, k, 0:EREST], v[EFULL * TP:E].rearrange("(p t) -> p t", p=1)).then_inc(s_edges, 16)
                sp.wait_ge(s_zero, 1)
                dmas = 0
                for table in m.sums:
                    flat = table.rearrange("n d -> (n d)")
                    for at in range(0, AGG * D, P * 2048):
                        k = min(P * 2048, AGG * D - at)
                        sp.dma_start(flat[at:at + k].rearrange("(p f) -> p f", p=P), zeros[:, 0:k // P]).then_inc(s_zeroed, 16)
                        dmas += 1
                sp.wait_ge(s_zeroed, 16 * dmas)

            @block.gpsimd
            def _(pool):
                nc.gpsimd.iota(iota_f[:], pattern=[[1, COLS]], base=0, channel_multiplier=0,
                               allow_small_or_imprecise_dtypes=True).then_inc(s_iota, 1)
                nc.gpsimd.iota(m.lane[:], pattern=[[0, 1]], base=TRASH, channel_multiplier=1,
                               allow_small_or_imprecise_dtypes=True).then_inc(s_iota, 1)
                nc.gpsimd.memset(m.ident[:], 1.0).then_inc(s_const, 1)
                nc.gpsimd.memset(m.upper[:], 1.0).then_inc(s_const, 1)
                pool.wait_ge(s_const, 2)
                nc.gpsimd.affine_select(out=m.ident[:], in_=m.ident[:], compare_op=ALU.is_equal, fill=0.0, base=0,
                                        pattern=[[1, P]], channel_multiplier=-1).then_inc(s_const, 1)
                nc.gpsimd.affine_select(out=m.upper[:], in_=m.upper[:], compare_op=ALU.is_gt, fill=0.0, base=0,
                                        pattern=[[1, P]], channel_multiplier=-1).then_inc(s_const, 1)

            @block.vector
            def _(dve):
                links = [0]

                def link(ins):
                    links[0] += 1
                    ins.then_inc(s_chain, 1)
                    dve.wait_ge(s_chain, links[0])

                nc.vector.memset(m.edge[:], -1).then_inc(s_pad, 1)
                nc.vector.memset(zeros[:], 0.0).then_inc(s_zero, 1)
                nc.vector.memset(m.eps[:], EPS)
                link(nc.vector.memset(zero_h[:], 0.0))
                dve.wait_ge(s_edges, 64)
                for k in range(2):
                    v = m.edge[:, k, :]
                    nc.vector.tensor_scalar(m.gather[:, k, :], v, 0, None, ALU.max)
                    link(nc.vector.tensor_scalar(ints[:, 0, :], v, 2, 127, ALU.arith_shift_right, ALU.bitwise_and))
                    link(nc.vector.tensor_copy(bins[:, 2 * k, :], ints[:, 0, :]))
                    link(nc.vector.tensor_scalar(ints[:, 1, :], v, 9, 2, ALU.arith_shift_right, ALU.arith_shift_left))
                    link(nc.vector.tensor_scalar(ints[:, 2, :], v, 3, None, ALU.bitwise_and))
                    link(nc.vector.tensor_tensor(ints[:, 3, :], ints[:, 1, :], ints[:, 2, :], ALU.add))
                    link(nc.vector.tensor_copy(bins[:, 2 * k + 1, :], ints[:, 3, :]))
                link(nc.vector.tensor_copy(m.dstf[:], m.edge[:, 1, :]))
                dve.wait_ge(s_iota, 2)
                link(nc.vector.tensor_copy(iota_h[:], iota_f[:]))

                def one_hots(i, first):
                    for k in range(2):
                        if not first:
                            dve.wait_ge(s_counted, i * 2 + (k - 1))
                        for u in range(8):
                            nc.vector.tensor_scalar(low[:, k, u, :], iota_h[:, 0:P], bins[:, 2 * k, bass.ds(i * 8 + u, 1)],
                                                    None, ALU.is_equal)
                            last = nc.vector.tensor_scalar(high[:, k, u, :], iota_h[:], bins[:, 2 * k + 1, bass.ds(i * 8 + u, 1)],
                                                           None, ALU.is_equal)
                        last.then_inc(s_hot, 1)

                one_hots(0, True)
                with dve.Fori(1, TP // 8) as i:
                    one_hots(i, False)
                dve.wait_ge(s_counted, 2 * (TP // 8) + 1)
                for k in range(2):
                    nc.vector.tensor_copy(m.deg[:, k, :], ps_hist[:, k, 0:COLS])
                    last = nc.vector.tensor_scalar(m.norm[:, k, :], ps_hist[:, k, 0:COLS], 1.0, None, ALU.max)
                last.then_inc(s_root, 1)
                dve.wait_ge(s_root, 2)
                nc.vector.reciprocal(m.norm[:], m.norm[:])

            @block.scalar
            def _(act):
                act.wait_ge(s_root, 1)
                nc.scalar.activation(m.norm[:], m.norm[:], ACT.Sqrt).then_inc(s_root, 1)

            @block.tensor
            def _(pe):
                pe.wait_ge(s_chain, 1)
                for k in range(2):
                    nc.tensor.matmul(ps_hist[:, k, 0:COLS], zero_h[:, 0:P], zero_h[:], start=True, stop=False)
                with pe.Fori(0, TP // 8) as i:
                    for k in range(2):
                        pe.wait_ge(s_hot, i * 2 + (k + 1))
                        for u in range(8):
                            last = nc.tensor.matmul(ps_hist[:, k, 0:COLS], low[:, k, u, :], high[:, k, u, :], start=False, stop=False)
                        last.then_inc(s_counted, 1)
                for k in range(2):
                    last = nc.tensor.matmul(ps_hist[:, k, 0:COLS], zero_h[:, 0:P], zero_h[:], start=False, stop=True)
                last.then_inc(s_counted, 1)


def weight_stage(nc, m, a):
    with ExitStack() as ctx:
        sem = lambda n: m.semaphore(nc, n)
        sb = lambda n, s, d: ctx.enter_context(nc.sbuf_tensor(m.tag + n, s, d))
        nat = sb("nat", [P, 9, P], F32)
        wt = sb("wt", [P, 9, P], F32)
        w2, wenc = sb("w2", [P, L, P], F32), sb("wenc", [P, P], F32)
        cols = sb("cols", [P, 10], F32)
        spread = sb("spread", [P, 5, P], F32)
        rows = sb("rows", [P, 5, P], F32)
        ps_t = ctx.enter_context(nc.psum_tensor(m.tag + "ps_t", [P, 3, 512], F32))
        ps_w = ctx.enter_context(nc.psum_tensor(m.tag + "ps_w", [P, 5, 512], F32))
        s_w, s_t, s_c, s_m, s_k = sem("s_w"), sem("s_t"), sem("s_c"), sem("s_m"), sem("s_k")
        col = lambda k: cols[:, k:k + 1]
        B2, LG, LB, GAMMA, BETA, BENC = 0, 2, 4, 6, 7, 8
        loads = [(m.w0[:], a["L0_gnn_W"]), (m.wres[:], a["L0_gnn_Wres"]), (nat[:, 8, :], a["L1_gnn_W_out"]),
                 (wenc[:], a["L1_gnn_W_enc"])]
        column = lambda v: v.rearrange("(d o) -> d o", o=1)
        row = lambda v: v.rearrange("(o d) -> o d", o=1).to_broadcast([P, D])
        for l in range(L):
            loads += [(nat[:, 4 * l:4 * l + 2, :], a["L1_gnn_msg_W1"][l].rearrange("o (k i) -> o k i", k=2)),
                      (nat[:, 4 * l + 2:4 * l + 4, :], a["L1_gnn_upd_W"][l].rearrange("o (k i) -> o k i", k=2)),
                      (w2[:, l, :], a["L1_gnn_msg_W2"][l]), (col(B2 + l), column(a["L1_gnn_msg_b2"][l])),
                      (col(LG + l), column(a["L1_gnn_ln_g"][l])), (col(LB + l), column(a["L1_gnn_ln_b"][l])),
                      (rows[:, 2 * l, :], row(a["L1_gnn_msg_b1"][l])), (rows[:, 2 * l + 1, :], row(a["L1_gnn_upd_b"][l]))]
        loads += [(col(GAMMA), column(a["L0_gnn_gamma"])), (col(BETA), column(a["L0_gnn_beta"])),
                  (col(BENC), column(a["L1_gnn_b_enc"])), (rows[:, 4, :], row(a["L1_gnn_b_out"]))]
        with nc.Block() as block:

            @block.sync
            def _(sp):
                for to, what in loads:
                    sp.dma_start(to, what).then_inc(s_w, 16)
                sp.wait_ge(s_w, 16 * len(loads))

            @block.tensor
            def _(pe):
                pe.wait_ge(s_w, 16 * len(loads))
                for k in range(9):
                    last = nc.tensor.transpose(ps_t[:, k // 4, (k % 4) * P:(k % 4 + 1) * P], nat[:, k, :], m.ident[:])
                last.then_inc(s_t, 1)
                pe.wait_ge(s_c, 1)
                p3 = lambda l: wt[:, 4 * l:4 * l + 3, :].rearrange("p k d -> p (k d)")
                nc.tensor.matmul(ps_w[:, 0, 0:384], wenc[:], p3(0), start=True, stop=True)
                nc.tensor.matmul(ps_w[:, 1, 0:384], spread[:, 0, :], p3(0), start=True, stop=True)
                nc.tensor.matmul(ps_w[:, 2, 0:384], spread[:, 1, :], p3(1), start=True, stop=True)
                nc.tensor.matmul(ps_w[:, 3, 0:128], spread[:, 2, :], wt[:, 8, :], start=True, stop=True)
                for l in range(L):
                    nc.tensor.matmul(ps_w[:, 4, l * 256:l * 256 + 128], w2[:, l, :], wt[:, 4 * l + 3, :], start=True, stop=True)
                    last = nc.tensor.matmul(ps_w[:, 4, l * 256 + 128:l * 256 + 256], spread[:, 3 + l, :], wt[:, 4 * l + 3, :],
                                            start=True, stop=True)
                last.then_inc(s_m, 1)

            @block.vector
            def _(dve):
                dve.wait_ge(s_w, 16 * len(loads))
                for k, c in enumerate((BENC, LB, LB + 1, B2, B2 + 1)):
                    nc.vector.tensor_copy(spread[:, k, :], col(c).to_broadcast([P, P]))
                nc.vector.tensor_copy(m.bn[:, 0:2], cols[:, GAMMA:GAMMA + 2])
                dve.wait_ge(s_t, 1)
                for k in range(9):
                    at = ps_t[:, k // 4, (k % 4) * P:(k % 4 + 1) * P]
                    if k % 4 == 2:
                        last = nc.vector.tensor_tensor(wt[:, k, :], at, m.ident[:], ALU.add)
                    else:
                        last = nc.vector.tensor_copy(wt[:, k, :], at)
                last.then_inc(s_c, 1)
                dve.wait_ge(s_c, 1)
                dve.wait_ge(s_m, 1)
                nc.vector.tensor_copy(m.wproj[:, 0, :], ps_w[:, 0, 0:384])
                nc.vector.tensor_scalar(m.wproj[:, 1, :], wt[:, 4:7, :].rearrange("p k d -> p (k d)"), col(LG), None, ALU.mult)
                nc.vector.tensor_scalar(m.wout[:], wt[:, 8, :], col(LG + 1), None, ALU.mult)
                nc.vector.tensor_tensor(m.bout[:], ps_w[:, 3, 0:128], rows[:, 4, :], ALU.add)
                for l in range(L):
                    nc.vector.tensor_copy(m.uw[:, l, :], ps_w[:, 4, l * 256:l * 256 + 128])
                    nc.vector.tensor_copy(m.ub2[:, l, :], ps_w[:, 4, l * 256 + 128:l * 256 + 256])
                    nc.vector.tensor_copy(m.bq[:, l, :], ps_w[:, 1 + l, 128:256])
                    nc.vector.tensor_tensor(m.bp[:, l, :], ps_w[:, 1 + l, 0:128], rows[:, 2 * l, :], ALU.add)
                    last = nc.vector.tensor_tensor(m.bu[:, l, :], ps_w[:, 1 + l, 256:384], rows[:, 2 * l + 1, :], ALU.add)
                last.then_inc(s_k, 1)
                dve.wait_ge(s_k, 1)
                for l in range(L):
                    nc.vector.tensor_tensor(m.bp[:, l, :], m.bp[:, l, :], m.bq[:, l, :], ALU.add)


def scale_stage(nc, m, x):
    R = 4
    with ExitStack() as ctx:
        sem = lambda n: m.semaphore(nc, n)
        sb = lambda n, s, d: ctx.enter_context(nc.sbuf_tensor(m.tag + n, s, d))
        xin, h = sb("xin", [P, R, CH], F32), sb("h", [P, R, CH], F32)
        s_x, s_out = [sem(f"s_x{r}") for r in range(R)], [sem(f"s_out{r}") for r in range(R)]
        s_h = sem("s_h")
        with nc.Block() as block:

            @block.sync
            def _(sp):
                def load(c, b, turn):
                    if not is_first(turn):
                        sp.wait_ge(s_h, c + (1 - R))
                    sp.dma_start(xin[0:parts(c), b, :], chunk_rows(x, c)).then_inc(s_x[b], 16)
                each_chunk(sp, R, load)

            @block.scalar
            def _(act):
                def store(c, b, turn):
                    act.wait_ge(s_h, c + 1)
                    act.dma_start(chunk(m.table_h, c), h[:, b, :]).then_inc(s_out[b], 16)
                each_chunk(act, R, store)
                for b in range(R):
                    act.wait_ge(s_out[b], 16 * slot_uses(R, b))

            @block.vector
            def _(dve):
                def scale(c, b, turn):
                    k = parts(c)
                    dve.wait_ge(s_x[b], turn * 16 + 16)
                    if not is_first(turn):
                        dve.wait_ge(s_out[b], turn * 16)
                    rows = lambda t: t[0:k, b, :].rearrange("p (j d) -> p j d", j=J)
                    nc.vector.tensor_tensor(rows(h), rows(xin),
                                            m.norm[0:k, 0, bass.ds(c * J, J)].unsqueeze(2).to_broadcast([k, J, D]),
                                            ALU.mult).then_inc(s_h, 1)
                each_chunk(dve, R, scale)


def edge_stage(nc, m, tables, sums, first_layer):
    K = len(tables)
    with ExitStack() as ctx:
        sem = lambda n: m.semaphore(nc, n)
        sb = lambda n, s, d: ctx.enter_context(nc.sbuf_tensor(m.tag + n, s, d))
        pb = lambda n, s, d: ctx.enter_context(nc.psum_tensor(m.tag + n, s, d))
        U = 2 * G
        rows = sb("rows", [P, K, U, D], F32)
        gidx = sb("gidx", [P, K, U], I32)
        sidx = sb("sidx", [P, U], I32)
        dcol = sb("dcol", [P, U], F32)
        same = sb("same", [P, U, P], F32)
        later = sb("later", [P, U, P], F32)
        count = sb("count", [P, U], F32)
        keep = sb("keep", [P, U], F32)
        total = sb("total", [P, U, D], F32)
        ps_d = pb("ps_d", [P, 2, G * P], F32)
        ps_m = pb("ps_m", [P, 2, G * P], F32)
        s_row = [[sem(f"s_row{k}_{u}") for u in range(U)] for k in range(K)]
        s_add = [sem("s_add_even"), sem("s_add_odd")]
        s_gidx, s_sidx, s_dcol, s_drow, s_same = sem("s_gidx"), sem("s_sidx"), sem("s_dcol"), sem("s_drow"), sem("s_same")
        s_sum, s_msg, s_merged, s_total, s_go = sem("s_sum"), sem("s_msg"), sem("s_merged"), sem("s_total"), sem("s_go")
        s_count, s_keep, s_masked = sem("s_count"), sem("s_keep"), sem("s_masked")
        with nc.Block() as block:

            @block.gpsimd
            def _(pool):
                def gather(k, h, j):
                    u = h * G + j
                    nc.gpsimd.indirect_dma_start(
                        out=rows[:, k, u, :], out_offset=None, in_=tables[k][:, :],
                        in_offset=bass.IndirectOffsetOnAxis(ap=gidx[:, k, u:u + 1], axis=0)).then_inc(s_row[k][u], 16)

                pool.wait_ge(s_gidx, 1)
                for j in range(G):
                    for k in range(K):
                        gather(k, 0, j)

                def group(g, h, turn):
                    more = not (isinstance(g, int) and g == NG - 1)
                    if more:
                        pool.wait_ge(s_gidx, g + 2)
                        if not (isinstance(g, int) and g == 0):
                            pool.wait_ge(s_merged, g)
                    for j in range(G):
                        u, parity = h * G + j, j % 2
                        if more:
                            if j == 0:
                                pool.sem_inc(s_go, 1)
                            for k in range(K):
                                gather(k, 1 - h, j)
                        if j == 0:
                            pool.wait_ge(s_sidx, g + 1)
                        pool.wait_ge(s_total, g * G + (j + 1))
                        if not (isinstance(g, int) and g == 0 and j < 2):
                            pool.wait_ge(s_add[parity], g * 32 + 16 * (j // 2))
                        pool.sem_inc(s_go, 1)
                        nc.gpsimd.indirect_dma_start(
                            out=sums[parity][:, :], out_offset=bass.IndirectOffsetOnAxis(ap=sidx[:, u:u + 1], axis=0),
                            in_=total[:, u, :], in_offset=None, compute_op=ALU.add).then_inc(s_add[parity], 16)
                each_group(pool, group)
                for parity in range(2):
                    pool.wait_ge(s_add[parity], 16 * TP // 2)

            @block.vector
            def _(dve):
                def give_gidx(g, h):
                    nc.vector.tensor_copy(gidx[:, :, h * G:h * G + G], m.gather[:, 0:K, bass.ds(g * G, G)]).then_inc(s_gidx, 1)

                def give_dcol(g, h):
                    nc.vector.tensor_copy(dcol[:, h * G:h * G + G], m.dstf[:, bass.ds(g * G, G)]).then_inc(s_dcol, 1)

                give_gidx(0, 0)
                give_gidx(1, 1)
                give_dcol(0, 0)

                def group(g, h, turn):
                    now = slice(h * G, h * G + G)
                    one_before_last = isinstance(g, int) and g >= NG - 2
                    dve.wait_ge(s_drow, g + 1)
                    dve.wait_ge(s_dcol, g + 1)
                    if not is_first(turn):
                        dve.wait_ge(s_merged, g - 1)
                    for j in range(G):
                        u = h * G + j
                        last = nc.vector.tensor_scalar(same[:, u, :], ps_d[:, h, j * P:(j + 1) * P], dcol[:, u:u + 1], None,
                                                       ALU.is_equal)
                        last.then_inc(s_same, 1)
                    if not is_first(turn):
                        for parity in range(2):
                            dve.wait_ge(s_add[parity], g * 32 - 32)
                    if first_layer:
                        for j in range(G):
                            u = h * G + j
                            dve.wait_ge(s_same, g * G + (j + 1))
                            nc.vector.tensor_tensor_reduce(out=later[:, u, :], in0=same[:, u, :], in1=m.upper[:], scale=1.0, scalar=0.0,
                                                           op0=ALU.mult, op1=ALU.add, accum_out=count[:, u:u + 1]).then_inc(s_count, 1)
                        dve.wait_ge(s_count, g * G + G)
                        nc.vector.tensor_scalar(count[:, now], count[:, now], 0.0, None, ALU.is_equal).then_inc(s_keep, 1)
                        dve.wait_ge(s_keep, g * 4 + 1)
                        nc.vector.scalar_tensor_tensor(out=keep[:, now], in0=dcol[:, now], scalar=0.0, in1=count[:, now],
                                                       op0=ALU.is_ge, op1=ALU.mult).then_inc(s_keep, 1)
                        dve.wait_ge(s_keep, g * 4 + 2)
                        nc.vector.scalar_tensor_tensor(out=count[:, now], in0=dcol[:, now], scalar=m.lane[:], in1=keep[:, now],
                                                       op0=ALU.subtract, op1=ALU.mult).then_inc(s_keep, 1)
                        dve.wait_ge(s_keep, g * 4 + 3)
                        nc.vector.tensor_scalar(sidx[:, now], count[:, now], m.lane[:], None, ALU.add).then_inc(s_keep, 1)
                        dve.wait_ge(s_keep, g * 4 + 4)
                        nc.vector.tensor_copy(m.target[:, bass.ds(g * G, G)], sidx[:, now]).then_inc(s_sidx, 1)
                    else:
                        nc.vector.tensor_copy(sidx[:, now], m.target[:, bass.ds(g * G, G)]).then_inc(s_sidx, 1)
                    if not (isinstance(g, int) and g == NG - 1):
                        if not (isinstance(g, int) and g == 0):
                            dve.wait_ge(s_same, g * G)
                        give_dcol(g + 1, 1 - h)
                    for j in range(G):
                        u = h * G + j
                        for k in range(K):
                            dve.wait_ge(s_row[k][u], turn * 16 + 16)
                        if K == 2:
                            nc.vector.tensor_tensor(rows[:, 0, u, :], rows[:, 0, u, :], rows[:, 1, u, :], ALU.add).then_inc(s_sum, 1)
                    if not one_before_last:
                        give_gidx(g + 2, h)
                each_group(dve, group)

            @block.scalar
            def _(act):
                def group(g, h, turn):
                    if K == 2:
                        for j in range(G):
                            u = h * G + j
                            act.wait_ge(s_sum, g * G + (j + 1))
                            nc.scalar.activation(rows[:, 0, u, :], rows[:, 0, u, :], ACT.Relu).then_inc(s_msg, 1)
                    act.wait_ge(s_merged, g + 1)
                    for j in range(G):
                        u = h * G + j
                        if not is_first(turn):
                            act.wait_ge(s_add[j % 2], g * 32 + (16 * (j // 2) - 48))
                        nc.scalar.copy(total[:, u, :], ps_m[:, h, j * P:(j + 1) * P]).then_inc(s_total, 1)
                each_group(act, group)

            @block.tensor
            def _(pe):
                def spread_targets(g, h):
                    pe.wait_ge(s_dcol, g + 1)
                    if not (isinstance(g, int) and g < 2):
                        pe.wait_ge(s_same, g * G - G)
                    for j in range(G):
                        u = h * G + j
                        last = nc.tensor.transpose(ps_d[:, h, j * P:(j + 1) * P], dcol[:, u:u + 1].to_broadcast([P, P]), m.ident[:])
                    last.then_inc(s_drow, 1)

                spread_targets(0, 0)

                def group(g, h, turn):
                    if not (isinstance(g, int) and g == NG - 1):
                        spread_targets(g + 1, 1 - h)
                    if not is_first(turn):
                        pe.wait_ge(s_total, g * G - G)
                    for j in range(G):
                        u = h * G + j
                        pe.wait_ge(s_same, g * G + (j + 1))
                        if K == 2:
                            pe.wait_ge(s_msg, g * G + (j + 1))
                        else:
                            pe.wait_ge(s_row[0][u], turn * 16 + 16)
                        last = nc.tensor.matmul(ps_m[:, h, j * P:(j + 1) * P], same[:, u, :], rows[:, 0, u, :], start=True, stop=True)
                    last.then_inc(s_merged, 1)
                each_group(pe, group)


def pipelined(eng, steps):
    lags = [lag for _, lag in steps]
    first = (2 + max(lags) + 1) // 2
    end = (NC - 1 + min(lags)) // 2

    def straight(steps_from, steps_to):
        for s in range(steps_from, steps_to):
            for body, lag in steps:
                if 0 <= s - lag < NC:
                    body(s - lag, (s - lag) % 2, (s - lag) // 2)

    straight(0, 2 * first)
    with eng.Fori(first, end) as i:
        for b in range(2):
            for body, lag in steps:
                body(i * 2 + (b - lag), (b - lag) % 2, i + (b - lag) // 2)
    straight(2 * end, NC + max(lags))


def conv_stage(nc, m, x):
    with ExitStack() as ctx:
        sem = lambda n: m.semaphore(nc, n)
        sb = lambda n: ctx.enter_context(nc.sbuf_tensor(m.tag + n, [P, 2, CH], F32))
        pb = lambda n: ctx.enter_context(nc.psum_tensor(m.tag + n, [P, 2, CH], F32))
        sum_a, sum_b, xin, agg, agg_t, x_t, relu_t, g_t = (sb(n) for n in ("sum_a", "sum_b", "xin", "agg", "agg_t", "x_t", "relu_t", "g_t"))
        ps_a, ps_x, ps_g, ps_r = (pb(n) for n in ("ps_a", "ps_x", "ps_g", "ps_r"))
        s_sa, s_sb, s_x, s_store = ([sem(f"{n}{b}") for b in range(2)] for n in ("s_sa", "s_sb", "s_x", "s_store"))
        s_pair, s_agg, s_flip_a, s_flip_x, s_agg_t, s_x_t = (sem(n) for n in ("s_pair", "s_agg", "s_flip_a", "s_flip_x", "s_agg_t", "s_x_t"))
        s_conv, s_res, s_relu, s_g, s_stat, s_pad = (sem(n) for n in ("s_conv", "s_res", "s_relu", "s_g", "s_stat", "s_pad"))
        rows = lambda t: t.rearrange("p (j d) -> p j d", j=J)
        with nc.Block() as block:

            @block.sync
            def _(sp):
                sp.wait_ge(s_pad, 1)

                def load(c, b, turn):
                    if not is_first(turn):
                        sp.wait_ge(s_agg, c - 1)
                    sp.dma_start(sum_a[:, b, :], chunk(m.sums[0], c)).then_inc(s_sa[b], 16)
                    sp.dma_start(sum_b[:, b, :], chunk(m.sums[1], c)).then_inc(s_sb[b], 16)
                    if not is_first(turn):
                        sp.wait_ge(s_flip_x, c - 1)
                    sp.dma_start(xin[0:parts(c), b, :], chunk_rows(x, c)).then_inc(s_x[b], 16)

                def store(c, b, turn):
                    sp.wait_ge(s_g, c + 1)
                    sp.dma_start(m.table_g[bass.ds(c * P, P), :], g_t[:, b, :]).then_inc(s_store[b], 16)
                pipelined(sp, [(load, 0), (store, 2)])
                for b in range(2):
                    sp.wait_ge(s_store[b], 16 * slot_uses(2, b))

            @block.gpsimd
            def _(pool):
                def pair(c, b, turn):
                    pool.wait_ge(s_sa[b], turn * 16 + 16)
                    pool.wait_ge(s_sb[b], turn * 16 + 16)
                    nc.gpsimd.tensor_tensor(sum_a[:, b, :], sum_a[:, b, :], sum_b[:, b, :], ALU.add).then_inc(s_pair, 1)
                pipelined(pool, [(pair, 0)])

            @block.vector
            def _(dve):
                nc.vector.memset(xin[:], 0.0).then_inc(s_pad, 1)

                def scale(c, b, turn):
                    dve.wait_ge(s_pair, c + 1)
                    if not is_first(turn):
                        dve.wait_ge(s_flip_a, c - 1)
                    nc.vector.tensor_tensor(rows(agg[:, b, :]), rows(sum_a[:, b, :]),
                                            m.norm[:, 1, bass.ds(c * J, J)].unsqueeze(2).to_broadcast([P, J, D]), ALU.mult).then_inc(s_agg, 1)

                def copy_x(c, b, turn):
                    dve.wait_ge(s_flip_x, c + 1)
                    if not is_first(turn):
                        dve.wait_ge(s_res, c - 1)
                    nc.vector.tensor_copy(x_t[:, b, :], ps_x[:, b, :]).then_inc(s_x_t, 1)

                def add(c, b, turn):
                    dve.wait_ge(s_res, c + 1)
                    dve.wait_ge(s_relu, c + 1)
                    if not is_first(turn):
                        dve.wait_ge(s_store[b], turn * 16)
                        dve.wait_ge(s_stat, c - 1)
                    nc.vector.scalar_tensor_tensor(out=g_t[:, b, :], in0=ps_r[:, b, :], scalar=0.0, in1=relu_t[:, b, :],
                                                   op0=ALU.max, op1=ALU.add).then_inc(s_g, 1)

                def stats(c, b, turn):
                    dve.wait_ge(s_g, c + 1)
                    if is_last(c):
                        for j in range(J):
                            last = nc.vector.bn_stats(m.stats[:, c + j, :], g_t[:, b, j * P:j * P + LAST])
                    else:
                        last = nc.vector.bn_stats(m.stats[:, bass.ds(c, 1), :].rearrange("p o s -> p (o s)"), g_t[:, b, :])
                    last.then_inc(s_stat, 1)
                pipelined(dve, [(scale, 0), (copy_x, 0), (add, 1), (stats, 1)])

            @block.scalar
            def _(act):
                def copy_agg(c, b, turn):
                    act.wait_ge(s_flip_a, c + 1)
                    if not is_first(turn):
                        act.wait_ge(s_conv, c - 1)
                    nc.scalar.copy(agg_t[:, b, :], ps_a[:, b, :]).then_inc(s_agg_t, 1)

                def relu(c, b, turn):
                    act.wait_ge(s_conv, c + 1)
                    if not is_first(turn):
                        act.wait_ge(s_g, c - 1)
                    nc.scalar.activation(relu_t[:, b, :], ps_g[:, b, :], ACT.Relu).then_inc(s_relu, 1)
                pipelined(act, [(copy_agg, 0), (relu, 1)])

            @block.tensor
            def _(pe):
                def flip(c, b, turn):
                    pe.wait_ge(s_x[b], turn * 16 + 16)
                    if not is_first(turn):
                        pe.wait_ge(s_x_t, c - 1)
                    for j in range(J):
                        last = nc.tensor.transpose(ps_x[:, b, j * P:(j + 1) * P], xin[:, b, j * P:(j + 1) * P], m.ident[:])
                    last.then_inc(s_flip_x, 1)
                    pe.wait_ge(s_agg, c + 1)
                    if not is_first(turn):
                        pe.wait_ge(s_agg_t, c - 1)
                    for j in range(J):
                        last = nc.tensor.transpose(ps_a[:, b, j * P:(j + 1) * P], agg[:, b, j * P:(j + 1) * P], m.ident[:])
                    last.then_inc(s_flip_a, 1)

                def products(c, b, turn):
                    pe.wait_ge(s_x_t, c + 1)
                    if not is_first(turn):
                        pe.wait_ge(s_g, c - 1)
                    nc.tensor.matmul(ps_r[:, b, :], m.wres[:], x_t[:, b, :], start=True, stop=True).then_inc(s_res, 1)
                    pe.wait_ge(s_agg_t, c + 1)
                    if not is_first(turn):
                        pe.wait_ge(s_relu, c - 1)
                    nc.tensor.matmul(ps_g[:, b, :], m.w0[:], agg_t[:, b, :], start=True, stop=True).then_inc(s_conv, 1)
                pipelined(pe, [(flip, 0), (products, 1)])


def node_stage(nc, m, x, out, layer):
    conv, final = layer < 0, layer == L - 1
    nxt = layer + 1
    with ExitStack() as ctx:
        sem = lambda n: m.semaphore(nc, n)
        sems = lambda n: [sem(f"{n}{b}") for b in range(2)]
        sb = lambda n: ctx.enter_context(nc.sbuf_tensor(m.tag + n, [P, 2, CH], F32))
        small = lambda n, k: ctx.enter_context(nc.sbuf_tensor(m.tag + n, [P, 2, J, k], F32))
        in_a, in_b, in_c = sb("in_a"), sb("in_b"), sb("in_c")
        y, z, z_t, flat_t = sb("y"), sb("z"), sb("z_t"), sb("flat_t")
        p_out, q_out, b_out, extra = sb("p_out"), sb("q_out"), sb("b_out"), sb("extra")
        v, res = sb("v"), sb("res")
        st, mv, rstd = small("st", 6), small("mv", 2), small("rstd", 1)
        st2, mv2, rstd2 = small("st2", 6), small("mv2", 2), small("rstd2", 1)
        coef = ctx.enter_context(nc.sbuf_tensor(m.tag + "coef", [P, 8], F32))
        pbank = lambda n, k: ctx.enter_context(nc.psum_tensor(m.tag + n, [P, k, CH], F32))
        ps_in, ps_u, ps_t, ps_pb, ps_q = pbank("ps_in", 2), pbank("ps_u", 1), pbank("ps_t", 1), pbank("ps_pb", 2), pbank("ps_q", 2)
        s_a, s_b, s_c = sems("s_a"), sems("s_b"), sems("s_c")
        s_store = {k: sems(f"s_store_{k}") for k in "xpqb"}
        (s_pad, s_coef, s_lift, s_pair, s_flip, s_sum_t, s_upd, s_y, s_stat, s_aggr, s_rstd, s_norm, s_flip_z, s_z_t, s_proj,
         s_out_p, s_out_q, s_out_b, s_extra_m, s_extra, s_v, s_stat2, s_aggr2, s_rstd2, s_res, s_std, s_std2, s_go, s_proj_q) = (sem(n) for n in (
             "s_pad", "s_coef", "s_lift", "s_pair", "s_flip", "s_sum_t", "s_upd", "s_y", "s_stat", "s_aggr", "s_rstd", "s_norm",
             "s_flip_z", "s_z_t", "s_proj", "s_out_p", "s_out_q", "s_out_b", "s_extra_m", "s_extra", "s_v", "s_stat2", "s_aggr2",
             "s_rstd2", "s_res", "s_std", "s_std2", "s_go", "s_proj_q"))
        rows = lambda t: t.rearrange("p (j d) -> p j d", j=J)
        over_j = lambda t: t.unsqueeze(1).to_broadcast([P, J, D])
        with nc.Block() as block:

            @block.sync
            def _(sp):
                if conv:
                    sp.wait_ge(s_pad, 1)

                def load(c, b, turn):
                    again = not is_first(turn)
                    if conv:
                        if again:
                            sp.wait_ge(s_lift, c - 1)
                        sp.dma_start(in_a[:, b, :], m.table_g[bass.ds(c * P, P), :]).then_inc(s_a[b], 16)
                        if again:
                            sp.wait_ge(s_y, c - 1)
                        sp.dma_start(in_b[0:parts(c), b, :], chunk_rows(x, c)).then_inc(s_b[b], 16)
                    else:
                        if again:
                            sp.wait_ge(s_flip, c - 1)
                        sp.dma_start(in_a[:, b, :], chunk(m.sums[2 * nxt], c)).then_inc(s_a[b], 16)
                        sp.dma_start(in_b[:, b, :], chunk(m.sums[2 * nxt + 1], c)).then_inc(s_b[b], 16)
                        if again:
                            sp.wait_ge(s_y, c - 1)
                        sp.dma_start(in_c[:, b, :], chunk(m.table_b[layer], c)).then_inc(s_c[b], 16)
                        if final:
                            if again:
                                sp.wait_ge(s_v, c - 1)
                            sp.dma_start(extra[:, b, :], chunk(m.table_x1, c)).then_inc(s_store["x"][b], 16)

                def store(c, b, turn):
                    if final:
                        sp.wait_ge(s_res, c * J + J)
                        sp.dma_start(chunk_rows(out, c), res[0:parts(c), b, :]).then_inc(s_store["b"][b], 16)
                        return
                    if conv:
                        sp.wait_ge(s_norm, c * J + J)
                        sp.dma_start(chunk(m.table_x1, c), z[:, b, :]).then_inc(s_store["x"][b], 16)
                    sp.wait_ge(s_out_p, c * 2 + 2)
                    sp.dma_start(chunk(m.table_p[nxt], c), p_out[:, b, :]).then_inc(s_store["p"][b], 16)
                    sp.wait_ge(s_out_b, c * 2 + 2)
                    sp.dma_start(chunk(m.table_b[nxt], c), b_out[:, b, :]).then_inc(s_store["b"][b], 16)
                pipelined(sp, [(load, 0), (store, 2)])
                for b in range(2):
                    for k in ("b",) if final else ("x", "p", "b") if conv else ("p", "b"):
                        sp.wait_ge(s_store[k][b], 16 * slot_uses(2, b))

            @block.gpsimd
            def _(pool):
                def pair(c, b, turn):
                    pool.wait_ge(s_a[b], turn * 16 + 16)
                    pool.wait_ge(s_b[b], turn * 16 + 16)
                    nc.gpsimd.tensor_tensor(in_a[:, b, :], in_a[:, b, :], in_b[:, b, :], ALU.add).then_inc(s_pair, 1)

                def add_extra(c, b, turn):
                    if final:
                        pool.wait_ge(s_store["x"][b], turn * 16 + 16)
                        nc.gpsimd.tensor_tensor(rows(extra[:, b, :]), rows(extra[:, b, :]), over_j(m.bout[:]), ALU.add).then_inc(s_extra, 1)
                        return
                    if not is_first(turn):
                        pool.wait_ge(s_out_b, c * 2 - 2)
                    nc.gpsimd.tensor_tensor(rows(extra[:, b, :]), over_j(m.ub2[:, nxt, :]),
                                            m.deg[:, 1, bass.ds(c * J, J)].unsqueeze(2).to_broadcast([P, J, D]), ALU.mult).then_inc(s_extra_m, 1)
                    pool.wait_ge(s_extra_m, c + 1)
                    nc.gpsimd.tensor_tensor(rows(extra[:, b, :]), rows(extra[:, b, :]), over_j(m.bu[:, nxt, :]), ALU.add).then_inc(s_extra, 1)

                def store_q(c, b, turn):
                    pool.wait_ge(s_out_q, c + 1)
                    pool.sem_inc(s_go, 1)
                    pool.dma_start(chunk(m.table_q[nxt], c), q_out[:, b, :]).then_inc(s_store["q"][b], 16)
                steps = ([] if conv else [(pair, 0)]) + [(add_extra, 0)] + ([] if final else [(store_q, 2)])
                pipelined(pool, steps)
                if not final:
                    for b in range(2):
                        pool.wait_ge(s_store["q"][b], 16 * slot_uses(2, b))

            @block.scalar
            def _(act):
                if conv:
                    act.wait_ge(s_coef, 1)
                    nc.scalar.activation(coef[:, 2:3], coef[:, 1:2], ACT.Sqrt, bias=m.eps[:]).then_inc(s_coef, 1)
                    act.wait_ge(s_coef, 6)

                def head(c, b, turn):
                    again = not is_first(turn)
                    if conv:
                        act.wait_ge(s_a[b], turn * 16 + 16)
                        if again:
                            act.wait_ge(s_flip, c - 1)
                        nc.scalar.activation(flat_t[:, b, :], in_a[:, b, :], ACT.Identity, scale=coef[:, 3:4],
                                             bias=coef[:, 5:6]).then_inc(s_lift, 1)
                    else:
                        act.wait_ge(s_flip, c + 1)
                        if again:
                            act.wait_ge(s_upd, c - 1)
                        nc.scalar.copy(flat_t[:, b, :], ps_in[:, b, :]).then_inc(s_sum_t, 1)

                def root(mv, rstd, s_aggr, s_std):
                    def body(c, b, turn):
                        act.wait_ge(s_aggr, c * J + J)
                        nc.scalar.activation(rstd[:, b, :, :], mv[:, b, :, 1:2], ACT.Sqrt, bias=m.eps[:]).then_inc(s_std, 1)
                    return body

                def copy_z(c, b, turn):
                    act.wait_ge(s_flip_z, c + 1)
                    if not is_first(turn):
                        act.wait_ge(s_proj_q if final else s_proj, c - 1 if final else c * 2 - 2)
                    nc.scalar.copy(z_t[:, b, :], ps_t[:, 0, :]).then_inc(s_z_t, 1)

                def evacuate_q(c, b, turn):
                    act.wait_ge(s_proj_q, c + 1)
                    if not is_first(turn):
                        act.wait_ge(s_store["q"][b], turn * 16)
                    nc.scalar.copy(q_out[:, b, :], ps_q[:, b, :]).then_inc(s_out_q, 1)
                pipelined(act, [(head, 0), (copy_z, 1), (root(mv, rstd, s_aggr, s_std), 0)]
                          + ([(root(mv2, rstd2, s_aggr2, s_std2), 1)] if final else [(evacuate_q, 1)]))

            @block.tensor
            def _(pe):
                def flip(c, b, turn):
                    again = not is_first(turn)
                    pe.wait_ge(s_lift if conv else s_pair, c + 1)
                    if again:
                        pe.wait_ge(s_y if conv else s_sum_t, c - 1)
                    what = flat_t if conv else in_a
                    for j in range(J):
                        last = nc.tensor.transpose(ps_in[:, b, j * P:(j + 1) * P], what[:, b, j * P:(j + 1) * P], m.ident[:])
                    last.then_inc(s_flip, 1)

                def update(c, b, turn):
                    pe.wait_ge(s_sum_t, c + 1)
                    if not (isinstance(c, int) and c == 0):
                        pe.wait_ge(s_y, c)
                    for j in range(J):
                        last = nc.tensor.matmul(ps_u[:, 0, j * D:(j + 1) * D], flat_t[:, b, j * P:(j + 1) * P], m.uw[:, layer, :],
                                                start=True, stop=True)
                    last.then_inc(s_upd, 1)

                def flip_z(c, b, turn):
                    pe.wait_ge(s_norm, c * J + J)
                    if not (isinstance(c, int) and c == 0):
                        pe.wait_ge(s_z_t, c)
                    for j in range(J):
                        last = nc.tensor.transpose(ps_t[:, 0, j * P:(j + 1) * P], z[:, b, j * P:(j + 1) * P], m.ident[:])
                    last.then_inc(s_flip_z, 1)

                def project(c, b, turn):
                    pe.wait_ge(s_z_t, c + 1)
                    if not is_first(turn):
                        pe.wait_ge(s_v if final else s_out_q, c - 1)
                    for j in range(J):
                        w = m.wout[:] if final else m.wproj[:, nxt, D:2 * D]
                        last = nc.tensor.matmul(ps_q[:, b, j * D:(j + 1) * D], z_t[:, b, j * P:(j + 1) * P], w, start=True, stop=True)
                    last.then_inc(s_proj_q, 1)
                    if final:
                        return
                    for h in range(2):
                        if not (isinstance(c, int) and c == 0):
                            pe.wait_ge(s_out_b, c * 2 + (h - 1))
                        for k in range(2):
                            j = 2 * h + k
                            last = nc.tensor.matmul(ps_pb[:, h, k * 2 * D:(k + 1) * 2 * D], z_t[:, b, j * P:(j + 1) * P],
                                                    m.wproj[:, nxt, :].rearrange("p (k d) -> p k d", k=3)[:, 0:3:2, :],
                                                    start=True, stop=True)
                        last.then_inc(s_proj, 1)
                pipelined(pe, [(flip, 0), (flip_z, 1)] + ([] if conv else [(update, 0)]) + [(project, 1)])

            @block.vector
            def _(dve):
                if conv:
                    links = [0]

                    def link(ins):
                        links[0] += 1
                        ins.then_inc(s_coef, 1)
                        dve.wait_ge(s_coef, links[0])
                    nc.vector.memset(in_b[:], 0.0).then_inc(s_pad, 1)
                    link(nc.vector.bn_aggr(coef[:, 0:2], m.stats[:].rearrange("p c s -> p (c s)")))
                    dve.wait_ge(s_coef, 2)
                    links[0] += 1
                    link(nc.vector.reciprocal(coef[:, 2:3], coef[:, 2:3]))
                    link(nc.vector.tensor_tensor(coef[:, 3:4], coef[:, 2:3], m.bn[:, 0:1], ALU.mult))
                    link(nc.vector.tensor_tensor(coef[:, 4:5], coef[:, 0:1], coef[:, 3:4], ALU.mult))
                    link(nc.vector.tensor_tensor(coef[:, 5:6], m.bn[:, 1:2], coef[:, 4:5], ALU.subtract))

                def make_y(c, b, turn):
                    if conv:
                        dve.wait_ge(s_flip, c + 1)
                        dve.wait_ge(s_b[b], turn * 16 + 16)
                    else:
                        dve.wait_ge(s_upd, c + 1)
                        dve.wait_ge(s_c[b], turn * 16 + 16)
                    nc.vector.tensor_tensor(y[:, b, :], ps_in[:, b, :] if conv else ps_u[:, 0, :],
                                            in_b[:, b, :] if conv else in_c[:, b, :], ALU.add).then_inc(s_y, 1)

                def measure(src, st, mv, ready, s_stat, s_aggr, c, b):
                    dve.wait_ge(ready, c + 1)
                    for j in range(J):
                        nc.vector.bn_stats(st[:, b, j, :], src[:, b, j * D:(j + 1) * D]).then_inc(s_stat, 1)
                    dve.wait_ge(s_stat, c * J + J)
                    dve.sem_inc(s_go, 1)
                    for j in range(J):
                        nc.vector.bn_aggr(mv[:, b, j, :], st[:, b, j, :]).then_inc(s_aggr, 1)

                def finish(src, dst, mv, rstd, s_std, s_rstd, s_done, c, b, free):
                    dve.wait_ge(s_std, c + 1)
                    nc.vector.reciprocal(rstd[:, b, :, :], rstd[:, b, :, :]).then_inc(s_rstd, 1)
                    free()
                    dve.wait_ge(s_rstd, c + 1)
                    for j in range(J):
                        nc.vector.tensor_scalar(dst[:, b, j * D:(j + 1) * D], src[:, b, j * D:(j + 1) * D], mv[:, b, j, 0:1],
                                                rstd[:, b, j, :], ALU.subtract, ALU.mult).then_inc(s_done, 1)

                def measure_y(c, b, turn):
                    measure(y, st, mv, s_y, s_stat, s_aggr, c, b)

                def norm_y(c, b, turn):
                    def free():
                        if not is_first(turn):
                            dve.wait_ge(s_flip_z, c - 1)
                            if conv:
                                dve.wait_ge(s_store["x"][b], turn * 16)
                    finish(y, z, mv, rstd, s_std, s_rstd, s_norm, c, b, free)

                def evacuate(c, b, turn):
                    for h in range(2):
                        dve.wait_ge(s_proj, c * 2 + (h + 1))
                        if h == 0:
                            if not is_first(turn):
                                dve.wait_ge(s_store["p"][b], turn * 16)
                                dve.wait_ge(s_store["b"][b], turn * 16)
                            dve.wait_ge(s_extra, c + 1)
                        two = slice(2 * h, 2 * h + 2)
                        both = ps_pb[:, h, :].rearrange("p (k t d) -> p k t d", k=2, t=2)
                        nc.vector.tensor_tensor(rows(p_out[:, b, :])[:, two, :], both[:, :, 0, :],
                                                m.bp[:, nxt, :].unsqueeze(1).to_broadcast([P, 2, D]), ALU.add).then_inc(s_out_p, 1)
                        nc.vector.tensor_tensor(rows(b_out[:, b, :])[:, two, :], both[:, :, 1, :],
                                                rows(extra[:, b, :])[:, two, :], ALU.add).then_inc(s_out_b, 1)

                def make_v(c, b, turn):
                    dve.wait_ge(s_proj_q, c + 1)
                    dve.wait_ge(s_extra, c + 1)
                    nc.vector.tensor_tensor(v[:, b, :], ps_q[:, b, :], extra[:, b, :], ALU.add).then_inc(s_v, 1)

                def measure_v(c, b, turn):
                    measure(v, st2, mv2, s_v, s_stat2, s_aggr2, c, b)

                def norm_v(c, b, turn):
                    def free():
                        if not is_first(turn):
                            dve.wait_ge(s_store["b"][b], turn * 16)
                    finish(v, res, mv2, rstd2, s_std2, s_rstd2, s_res, c, b, free)
                pipelined(dve, [(make_y, 0), (measure_y, 0)] + ([(make_v, 1), (measure_v, 1), (norm_y, 0), (norm_v, 1)] if final
                                                               else [(evacuate, 1), (norm_y, 0)]))


def build(nc, a, out):
    m = Mem()
    table = lambda n, r, w: nc.dram_tensor(n, [r, w], F32, kind="Internal").ap()
    m.table_h, m.table_x1 = table("table_h", NPAD, D), table("table_x1", NPAD, D)
    m.table_g = table("table_g", NC * P, CH)
    m.table_p, m.table_q, m.table_b = ([table(f"table_{k}{l}", NPAD, D) for l in range(L)] for k in "pqb")
    m.sums = [table(f"sums{k}", AGG, D) for k in range(2 * (L + 1))]
    with ExitStack() as ctx:
        sb = lambda n, s, d=F32: ctx.enter_context(nc.sbuf_tensor(n, s, d))
        m.edge, m.gather = sb("edge", [P, 2, TP], I32), sb("gather", [P, 2, TP], I32)
        m.target, m.dstf = sb("target", [P, TP], I32), sb("dstf", [P, TP])
        m.deg, m.norm = sb("deg", [P, 2, COLS]), sb("norm", [P, 2, COLS])
        m.ident, m.upper, m.lane, m.eps = sb("ident", [P, P]), sb("upper", [P, P]), sb("lane", [P, 1]), sb("eps", [P, 1])
        m.w0, m.wres, m.wproj, m.wout = sb("w0", [P, D]), sb("wres", [P, D]), sb("wproj", [P, L, 3 * D]), sb("wout", [P, D])
        m.uw, m.ub2 = sb("uw", [P, L, D]), sb("ub2", [P, L, D])
        m.bp, m.bq, m.bu, m.bout, m.bn = sb("bp", [P, L, D]), sb("bq", [P, L, D]), sb("bu", [P, L, D]), sb("bout", [P, D]), sb("bn", [P, 2])
        m.stats = sb("stats", [P, NC - 1 + J, 6])
        def stage(name, make, *args):
            m.tag, m.sems = name + "_", []
            make(nc, m, *args)
            nc.clear_and_free_semaphores(m.sems)
            nc.all_engine_barrier()
        stage("setup", setup_stage, a)
        stage("weights", weight_stage, a)
        stage("scale", scale_stage, a["x"])
        stage("edges", edge_stage, [m.table_h], m.sums[0:2], True)
        stage("conv", conv_stage, a["x"])
        stage("nodes", node_stage, a["x"], out, -1)
        for l in range(L):
            stage(f"edges{l}", edge_stage, [m.table_p[l], m.table_q[l]], m.sums[2 * l + 2:2 * l + 4], False)
            stage(f"nodes{l}", node_stage, a["x"], out, l)


def kernel(**inputs):
    import numpy as np
    import concourse.bacc as bacc
    from concourse.bass_utils import run_bass_kernel_spmd as run
    nc = bacc.Bacc("TRN2", target_bir_lowering=False, num_devices=1)
    arrays, a = {}, {}
    for name, value in inputs.items():
        value = np.ascontiguousarray(value)
        arrays[f"in_{name}"] = value
        a[name] = nc.dram_tensor(f"in_{name}", value.shape, mybir.dt.from_np(value.dtype), kind="ExternalInput").ap()
    out = nc.dram_tensor("out_0", (N, D), F32, kind="ExternalOutput").ap()
    build(nc, a, out)
    return run(nc, [arrays], core_ids=[0]).results[0]["out_0"]
```

```python
from contextlib import ExitStack

import concourse.bass as bass
from concourse import mybir

F32, F16, I32 = mybir.dt.float32, mybir.dt.float16, mybir.dt.int32
ALU, ACT, AX = mybir.AluOpType, mybir.ActivationFunctionType, mybir.AxisListType

P = 128
N, E, D, L = 50000, 50000, 128, 2
J = 4
CH = P * J
NC = -(-N // CH)
NPAD = NC * CH
LAST = (N - (NC - 1) * CH) // J
COLS = NC * J
TP = 392
EFULL = E // TP
EREST = E - EFULL * TP
G = 4
NG = TP // G
TRASH = NPAD
AGG = NPAD + P
EPS = 1e-5


class Mem:

    def semaphore(self, nc, name):
        self.sems.append(nc.alloc_semaphore(self.tag + name))
        return self.sems[-1]


def chunk(table, c):
    return table[bass.ds(c * CH, CH), :].rearrange("(p j) d -> p (j d)", j=J)


def chunk_rows(table, c):
    if is_last(c):
        return table[c * CH:N, :].rearrange("(p j) d -> p (j d)", j=J)
    return chunk(table, c)


def each_chunk(eng, ring, body):
    turns = (NC - 1) // ring
    for b in range(ring):
        body(b, b, 0)
    with eng.Fori(1, turns) as i:
        for b in range(ring):
            body(i * ring + b, b, i)
    for c in range(turns * ring, NC):
        body(c, c % ring, c // ring)


def each_group(eng, body):
    turns = NG // 2
    for h in range(2):
        body(h, h, 0)
    with eng.Fori(1, turns - 1) as i:
        for h in range(2):
            body(i * 2 + h, h, i)
    for h in range(2):
        body(NG - 2 + h, h, turns - 1)


def is_first(turn):
    return isinstance(turn, int) and turn == 0


def is_last(c):
    return isinstance(c, int) and c == NC - 1


def parts(c):
    return LAST if is_last(c) else P


def slot_uses(ring, b):
    return len(range(b, NC, ring))


def zero_tables(m, eng, tables, done, pace=None):
    dmas = 0
    for table in tables:
        flat = table.rearrange("n d -> (n d)")
        step = P * (2048 if pace is None else 512)
        for at in range(0, AGG * D, step):
            k = min(step, AGG * D - at)
            if pace is not None and dmas % 4 == 0:
                eng.wait_ge(pace, min(dmas // 4 + 1, NG))
            eng.dma_start(flat[at:at + k].rearrange("(p f) -> p f", p=P), m.zeros[:, 0:k // P]).then_inc(done, 16)
            dmas += 1
    eng.wait_ge(done, 16 * dmas)


def one_hot(nc, m, k, tile, low, high):
    nc.vector.tensor_scalar(low, m.iota[:, 0:P], m.bins[:, 2 * k, bass.ds(tile, 1)], None, ALU.is_equal)
    return nc.vector.tensor_scalar(high, m.iota[:], m.bins[:, 2 * k + 1, bass.ds(tile, 1)], None, ALU.is_equal)


def finish_degrees(nc, m, dve, k, ps_hist, s_root):
    nc.vector.tensor_copy(m.deg[:, k, :], ps_hist[:, 0:COLS])
    nc.vector.tensor_scalar(m.norm[:, k, :], ps_hist[:, 0:COLS], 1.0, None, ALU.max).then_inc(s_root, 1)
    dve.wait_ge(s_root, 2)
    nc.vector.reciprocal(m.norm[:, k, :], m.norm[:, k, :])


def setup_stage(nc, m, a):
    with ExitStack() as ctx:
        sem = lambda n: m.semaphore(nc, n)
        sb = lambda n, s, d: ctx.enter_context(nc.sbuf_tensor(m.tag + n, s, d))
        pb = lambda n, s, d: ctx.enter_context(nc.psum_tensor(m.tag + n, s, d))
        iota_f = sb("iota_f", [P, COLS], F32)
        ints = sb("ints", [P, 4, TP], I32)
        low = sb("low", [P, 2, 8, P], F16)
        high = sb("high", [P, 2, 8, COLS], F16)
        ps_hist = pb("ps_hist", [P, 512], F32)
        s_pad, s_edges, s_iota, s_const = sem("s_pad"), sem("s_edges"), sem("s_iota"), sem("s_const")
        s_zero, s_zeroed = sem("s_zero"), sem("s_zeroed")
        s_chain, s_hot, s_counted, s_root = sem("s_chain"), sem("s_hot"), sem("s_counted"), sem("s_root")
        with nc.Block() as block:

            @block.sync
            def _(sp):
                sp.wait_ge(s_pad, 1)
                for k, v in enumerate((a["src"], a["dst"])):
                    sp.dma_start(m.edge[0:EFULL, k, :], v[0:EFULL * TP].rearrange("(p t) -> p t", t=TP)).then_inc(s_edges, 16)
                    sp.dma_start(m.edge[EFULL:P, k, 0:EREST], v[EFULL * TP:E].rearrange("(p t) -> p t", p=1)).then_inc(s_edges, 16)
                sp.wait_ge(s_zero, 1)
                zero_tables(m, sp, m.sums[0:2], s_zeroed)

            @block.gpsimd
            def _(pool):
                nc.gpsimd.iota(iota_f[:], pattern=[[1, COLS]], base=0, channel_multiplier=0,
                               allow_small_or_imprecise_dtypes=True).then_inc(s_iota, 1)
                nc.gpsimd.iota(m.lane[:], pattern=[[0, 1]], base=TRASH, channel_multiplier=1,
                               allow_small_or_imprecise_dtypes=True).then_inc(s_iota, 1)
                nc.gpsimd.memset(m.ident[:], 1.0).then_inc(s_const, 1)
                nc.gpsimd.memset(m.upper[:], 1.0).then_inc(s_const, 1)
                pool.wait_ge(s_const, 2)
                nc.gpsimd.affine_select(out=m.ident[:], in_=m.ident[:], compare_op=ALU.is_equal, fill=0.0, base=0,
                                        pattern=[[1, P]], channel_multiplier=-1).then_inc(s_const, 1)
                nc.gpsimd.affine_select(out=m.upper[:], in_=m.upper[:], compare_op=ALU.is_gt, fill=0.0, base=0,
                                        pattern=[[1, P]], channel_multiplier=-1).then_inc(s_const, 1)

            @block.vector
            def _(dve):
                links = [0]

                def link(ins):
                    links[0] += 1
                    ins.then_inc(s_chain, 1)
                    dve.wait_ge(s_chain, links[0])

                nc.vector.memset(m.edge[:], -1).then_inc(s_pad, 1)
                nc.vector.memset(m.zeros[:], 0.0).then_inc(s_zero, 1)
                nc.vector.memset(m.eps[:], EPS)
                link(nc.vector.memset(m.zero_h[:], 0.0))
                dve.wait_ge(s_edges, 64)
                for k in range(2):
                    v = m.edge[:, k, :]
                    nc.vector.tensor_scalar(m.gather[:, k, :], v, 0, None, ALU.max)
                    link(nc.vector.tensor_scalar(ints[:, 0, :], v, 2, 127, ALU.arith_shift_right, ALU.bitwise_and))
                    link(nc.vector.tensor_copy(m.bins[:, 2 * k, :], ints[:, 0, :]))
                    link(nc.vector.tensor_scalar(ints[:, 1, :], v, 9, 2, ALU.arith_shift_right, ALU.arith_shift_left))
                    link(nc.vector.tensor_scalar(ints[:, 2, :], v, 3, None, ALU.bitwise_and))
                    link(nc.vector.tensor_tensor(ints[:, 3, :], ints[:, 1, :], ints[:, 2, :], ALU.add))
                    link(nc.vector.tensor_copy(m.bins[:, 2 * k + 1, :], ints[:, 3, :]))
                link(nc.vector.tensor_copy(m.dstf[:], m.edge[:, 1, :]))
                dve.wait_ge(s_iota, 2)
                link(nc.vector.tensor_copy(m.iota[:], iota_f[:]))

                def one_hots(i, first):
                    for h in range(2):
                        if not first:
                            dve.wait_ge(s_counted, i * 2 + (h - 1))
                        for u in range(8):
                            last = one_hot(nc, m, 0, i * 16 + (8 * h + u), low[:, h, u, :], high[:, h, u, :])
                        last.then_inc(s_hot, 1)

                one_hots(0, True)
                with dve.Fori(1, TP // 16) as i:
                    one_hots(i, False)
                dve.wait_ge(s_counted, TP // 8 - 2)
                for u in range(8):
                    last = one_hot(nc, m, 0, TP - 8 + u, low[:, 0, u, :], high[:, 0, u, :])
                last.then_inc(s_hot, 1)
                dve.wait_ge(s_counted, TP // 8 + 1)
                finish_degrees(nc, m, dve, 0, ps_hist, s_root)

            @block.scalar
            def _(act):
                act.wait_ge(s_root, 1)
                nc.scalar.activation(m.norm[:, 0, :], m.norm[:, 0, :], ACT.Sqrt).then_inc(s_root, 1)

            @block.tensor
            def _(pe):
                pe.wait_ge(s_chain, 1)
                nc.tensor.matmul(ps_hist[:, 0:COLS], m.zero_h[:, 0:P], m.zero_h[:], start=True, stop=False)

                def count(turn, h):
                    pe.wait_ge(s_hot, turn + 1)
                    for u in range(8):
                        last = nc.tensor.matmul(ps_hist[:, 0:COLS], low[:, h, u, :], high[:, h, u, :], start=False, stop=False)
                    last.then_inc(s_counted, 1)
                with pe.Fori(0, TP // 16) as i:
                    for h in range(2):
                        count(i * 2 + h, h)
                count(TP // 8 - 1, 0)
                nc.tensor.matmul(ps_hist[:, 0:COLS], m.zero_h[:, 0:P], m.zero_h[:], start=False, stop=True).then_inc(s_counted, 1)


def weight_stage(nc, m, a):
    with ExitStack() as ctx:
        sem = lambda n: m.semaphore(nc, n)
        sb = lambda n, s, d: ctx.enter_context(nc.sbuf_tensor(m.tag + n, s, d))
        nat = sb("nat", [P, 9, P], F32)
        wt = sb("wt", [P, 9, P], F32)
        w2, wenc = sb("w2", [P, L, P], F32), sb("wenc", [P, P], F32)
        cols = sb("cols", [P, 10], F32)
        spread = sb("spread", [P, 5, P], F32)
        rows = sb("rows", [P, 5, P], F32)
        ps_t = ctx.enter_context(nc.psum_tensor(m.tag + "ps_t", [P, 3, 512], F32))
        ps_w = ctx.enter_context(nc.psum_tensor(m.tag + "ps_w", [P, 5, 512], F32))
        s_w, s_t, s_c, s_m, s_k = sem("s_w"), sem("s_t"), sem("s_c"), sem("s_m"), sem("s_k")
        col = lambda k: cols[:, k:k + 1]
        B2, LG, LB, GAMMA, BETA, BENC = 0, 2, 4, 6, 7, 8
        loads = [(m.w0[:], a["L0_gnn_W"]), (m.wres[:], a["L0_gnn_Wres"]), (nat[:, 8, :], a["L1_gnn_W_out"]),
                 (wenc[:], a["L1_gnn_W_enc"])]
        column = lambda v: v.rearrange("(d o) -> d o", o=1)
        row = lambda v: v.rearrange("(o d) -> o d", o=1).to_broadcast([P, D])
        for l in range(L):
            loads += [(nat[:, 4 * l:4 * l + 2, :], a["L1_gnn_msg_W1"][l].rearrange("o (k i) -> o k i", k=2)),
                      (nat[:, 4 * l + 2:4 * l + 4, :], a["L1_gnn_upd_W"][l].rearrange("o (k i) -> o k i", k=2)),
                      (w2[:, l, :], a["L1_gnn_msg_W2"][l]), (col(B2 + l), column(a["L1_gnn_msg_b2"][l])),
                      (col(LG + l), column(a["L1_gnn_ln_g"][l])), (col(LB + l), column(a["L1_gnn_ln_b"][l])),
                      (rows[:, 2 * l, :], row(a["L1_gnn_msg_b1"][l])), (rows[:, 2 * l + 1, :], row(a["L1_gnn_upd_b"][l]))]
        loads += [(col(GAMMA), column(a["L0_gnn_gamma"])), (col(BETA), column(a["L0_gnn_beta"])),
                  (col(BENC), column(a["L1_gnn_b_enc"])), (rows[:, 4, :], row(a["L1_gnn_b_out"]))]
        with nc.Block() as block:

            @block.sync
            def _(sp):
                for to, what in loads:
                    sp.dma_start(to, what).then_inc(s_w, 16)
                sp.wait_ge(s_w, 16 * len(loads))

            @block.tensor
            def _(pe):
                pe.wait_ge(s_w, 16 * len(loads))
                for k in range(9):
                    last = nc.tensor.transpose(ps_t[:, k // 4, (k % 4) * P:(k % 4 + 1) * P], nat[:, k, :], m.ident[:])
                last.then_inc(s_t, 1)
                pe.wait_ge(s_c, 1)
                p3 = lambda l: wt[:, 4 * l:4 * l + 3, :].rearrange("p k d -> p (k d)")
                nc.tensor.matmul(ps_w[:, 0, 0:384], wenc[:], p3(0), start=True, stop=True)
                nc.tensor.matmul(ps_w[:, 1, 0:384], spread[:, 0, :], p3(0), start=True, stop=True)
                nc.tensor.matmul(ps_w[:, 2, 0:384], spread[:, 1, :], p3(1), start=True, stop=True)
                nc.tensor.matmul(ps_w[:, 3, 0:128], spread[:, 2, :], wt[:, 8, :], start=True, stop=True)
                for l in range(L):
                    nc.tensor.matmul(ps_w[:, 4, l * 256:l * 256 + 128], w2[:, l, :], wt[:, 4 * l + 3, :], start=True, stop=True)
                    last = nc.tensor.matmul(ps_w[:, 4, l * 256 + 128:l * 256 + 256], spread[:, 3 + l, :], wt[:, 4 * l + 3, :],
                                            start=True, stop=True)
                last.then_inc(s_m, 1)

            @block.vector
            def _(dve):
                dve.wait_ge(s_w, 16 * len(loads))
                for k, c in enumerate((BENC, LB, LB + 1, B2, B2 + 1)):
                    nc.vector.tensor_copy(spread[:, k, :], col(c).to_broadcast([P, P]))
                nc.vector.tensor_copy(m.bn[:, 0:2], cols[:, GAMMA:GAMMA + 2])
                dve.wait_ge(s_t, 1)
                for k in range(9):
                    at = ps_t[:, k // 4, (k % 4) * P:(k % 4 + 1) * P]
                    if k % 4 == 2:
                        last = nc.vector.tensor_tensor(wt[:, k, :], at, m.ident[:], ALU.add)
                    else:
                        last = nc.vector.tensor_copy(wt[:, k, :], at)
                last.then_inc(s_c, 1)
                dve.wait_ge(s_c, 1)
                dve.wait_ge(s_m, 1)
                nc.vector.tensor_copy(m.wproj[:, 0, :], ps_w[:, 0, 0:384])
                nc.vector.tensor_scalar(m.wproj[:, 1, :], wt[:, 4:7, :].rearrange("p k d -> p (k d)"), col(LG), None, ALU.mult)
                nc.vector.tensor_scalar(m.wout[:], wt[:, 8, :], col(LG + 1), None, ALU.mult)
                nc.vector.tensor_tensor(m.bout[:], ps_w[:, 3, 0:128], rows[:, 4, :], ALU.add)
                for l in range(L):
                    nc.vector.tensor_copy(m.uw[:, l, :], ps_w[:, 4, l * 256:l * 256 + 128])
                    nc.vector.tensor_copy(m.ub2[:, l, :], ps_w[:, 4, l * 256 + 128:l * 256 + 256])
                    nc.vector.tensor_copy(m.bq[:, l, :], ps_w[:, 1 + l, 128:256])
                    nc.vector.tensor_tensor(m.bp[:, l, :], ps_w[:, 1 + l, 0:128], rows[:, 2 * l, :], ALU.add)
                    last = nc.vector.tensor_tensor(m.bu[:, l, :], ps_w[:, 1 + l, 256:384], rows[:, 2 * l + 1, :], ALU.add)
                last.then_inc(s_k, 1)
                dve.wait_ge(s_k, 1)
                for l in range(L):
                    nc.vector.tensor_tensor(m.bp[:, l, :], m.bp[:, l, :], m.bq[:, l, :], ALU.add)


def scale_stage(nc, m, x):
    R = 4
    with ExitStack() as ctx:
        sem = lambda n: m.semaphore(nc, n)
        sb = lambda n, s, d: ctx.enter_context(nc.sbuf_tensor(m.tag + n, s, d))
        xin, h = sb("xin", [P, R, CH], F32), sb("h", [P, R, CH], F32)
        s_x, s_out = [sem(f"s_x{r}") for r in range(R)], [sem(f"s_out{r}") for r in range(R)]
        s_h = sem("s_h")
        with nc.Block() as block:

            @block.sync
            def _(sp):
                def load(c, b, turn):
                    if not is_first(turn):
                        sp.wait_ge(s_h, c + (1 - R))
                    sp.dma_start(xin[0:parts(c), b, :], chunk_rows(x, c)).then_inc(s_x[b], 16)
                each_chunk(sp, R, load)

            @block.scalar
            def _(act):
                def store(c, b, turn):
                    act.wait_ge(s_h, c + 1)
                    act.dma_start(chunk(m.table_h, c), h[:, b, :]).then_inc(s_out[b], 16)
                each_chunk(act, R, store)
                for b in range(R):
                    act.wait_ge(s_out[b], 16 * slot_uses(R, b))

            @block.vector
            def _(dve):
                def scale(c, b, turn):
                    k = parts(c)
                    dve.wait_ge(s_x[b], turn * 16 + 16)
                    if not is_first(turn):
                        dve.wait_ge(s_out[b], turn * 16)
                    rows = lambda t: t[0:k, b, :].rearrange("p (j d) -> p j d", j=J)
                    nc.vector.tensor_tensor(rows(h), rows(xin),
                                            m.norm[0:k, 0, bass.ds(c * J, J)].unsqueeze(2).to_broadcast([k, J, D]),
                                            ALU.mult).then_inc(s_h, 1)
                each_chunk(dve, R, scale)


def edge_stage(nc, m, tables, sums, later_sums, first_layer):
    K = len(tables)
    LEAD = 2
    with ExitStack() as ctx:
        sem = lambda n: m.semaphore(nc, n)
        sb = lambda n, s, d: ctx.enter_context(nc.sbuf_tensor(m.tag + n, s, d))
        pb = lambda n, s, d: ctx.enter_context(nc.psum_tensor(m.tag + n, s, d))
        U = 2 * G
        rows = sb("rows", [P, K, U, D], F32)
        gidx = sb("gidx", [P, K, U], I32)
        sidx = sb("sidx", [P, U], I32)
        dcol = sb("dcol", [P, U], F32)
        same = sb("same", [P, U, P], F32)
        later = sb("later", [P, U, P], F32)
        count = sb("count", [P, U], F32)
        keep = sb("keep", [P, U], F32)
        total = sb("total", [P, U, D], F32)
        ps_d = pb("ps_d", [P, 2, G * P], F32)
        ps_m = pb("ps_m", [P, 2, G * P], F32)
        s_row = [[sem(f"s_row{k}_{u}") for u in range(U)] for k in range(K)]
        s_add = [sem("s_add_even"), sem("s_add_odd")]
        s_gidx, s_sidx, s_dcol, s_drow, s_same = sem("s_gidx"), sem("s_sidx"), sem("s_dcol"), sem("s_drow"), sem("s_same")
        s_sum, s_msg, s_merged, s_total, s_go = sem("s_sum"), sem("s_msg"), sem("s_merged"), sem("s_total"), sem("s_go")
        s_count, s_keep = sem("s_count"), sem("s_keep")
        low, high = sb("low", [P, U, P], F16), sb("high", [P, U, COLS], F16)
        ps_hist = pb("ps_hist", [P, 512], F32)
        s_hot, s_counted, s_root, s_zeroed = sem("s_hot"), sem("s_counted"), sem("s_root"), sem("s_zeroed")
        with nc.Block() as block:

            @block.sync
            def _(sp):
                if first_layer:
                    zero_tables(m, sp, later_sums, s_zeroed, s_merged)

            @block.gpsimd
            def _(pool):
                def gather(k, h, j):
                    u = h * G + j
                    nc.gpsimd.indirect_dma_start(
                        out=rows[:, k, u, :], out_offset=None, in_=tables[k][:, :],
                        in_offset=bass.IndirectOffsetOnAxis(ap=gidx[:, k, u:u + 1], axis=0)).then_inc(s_row[k][u], 16)

                pool.wait_ge(s_gidx, 1)
                for j in range(G):
                    for k in range(K):
                        gather(k, 0, j)

                def group(g, h, turn):
                    more = not (isinstance(g, int) and g == NG - 1)
                    if more:
                        pool.wait_ge(s_gidx, g + 2)
                        if not (isinstance(g, int) and g == 0):
                            pool.wait_ge(s_merged, g)
                    def gathers(j):
                        if more and j < G:
                            if j == 0:
                                pool.sem_inc(s_go, 1)
                            for k in range(K):
                                gather(k, 1 - h, j)
                    for j in range(LEAD):
                        gathers(j)
                    for j in range(G):
                        u, parity = h * G + j, j % 2
                        if j == 0:
                            pool.wait_ge(s_sidx, g + 1)
                        pool.wait_ge(s_total, g * G + (j + 1))
                        if not (isinstance(g, int) and g == 0 and j < 2):
                            pool.wait_ge(s_add[parity], g * 32 + 16 * (j // 2))
                        pool.sem_inc(s_go, 1)
                        nc.gpsimd.indirect_dma_start(
                            out=sums[parity][:, :], out_offset=bass.IndirectOffsetOnAxis(ap=sidx[:, u:u + 1], axis=0),
                            in_=total[:, u, :], in_offset=None, compute_op=ALU.add).then_inc(s_add[parity], 16)
                        gathers(j + LEAD)
                each_group(pool, group)
                for parity in range(2):
                    pool.wait_ge(s_add[parity], 16 * TP // 2)

            @block.vector
            def _(dve):
                def give_gidx(g, h):
                    nc.vector.tensor_copy(gidx[:, :, h * G:h * G + G], m.gather[:, 0:K, bass.ds(g * G, G)]).then_inc(s_gidx, 1)

                def give_dcol(g, h):
                    nc.vector.tensor_copy(dcol[:, h * G:h * G + G], m.dstf[:, bass.ds(g * G, G)]).then_inc(s_dcol, 1)

                give_gidx(0, 0)
                give_gidx(1, 1)
                give_dcol(0, 0)

                def group(g, h, turn):
                    now = slice(h * G, h * G + G)
                    one_before_last = isinstance(g, int) and g >= NG - 2
                    dve.wait_ge(s_drow, g + 1)
                    dve.wait_ge(s_dcol, g + 1)
                    if not is_first(turn):
                        dve.wait_ge(s_merged, g - 1)
                    for j in range(G):
                        u = h * G + j
                        last = nc.vector.tensor_scalar(same[:, u, :], ps_d[:, h, j * P:(j + 1) * P], dcol[:, u:u + 1], None,
                                                       ALU.is_equal)
                        last.then_inc(s_same, 1)
                    if not is_first(turn):
                        for parity in range(2):
                            dve.wait_ge(s_add[parity], g * 32 - 32)
                    if first_layer:
                        for j in range(G):
                            u = h * G + j
                            dve.wait_ge(s_same, g * G + (j + 1))
                            nc.vector.tensor_tensor_reduce(out=later[:, u, :], in0=same[:, u, :], in1=m.upper[:], scale=1.0, scalar=0.0,
                                                           op0=ALU.mult, op1=ALU.add, accum_out=count[:, u:u + 1]).then_inc(s_count, 1)
                        dve.wait_ge(s_count, g * G + G)
                        nc.vector.tensor_scalar(count[:, now], count[:, now], 0.0, None, ALU.is_equal).then_inc(s_keep, 1)
                        dve.wait_ge(s_keep, g * 4 + 1)
                        nc.vector.scalar_tensor_tensor(out=keep[:, now], in0=dcol[:, now], scalar=0.0, in1=count[:, now],
                                                       op0=ALU.is_ge, op1=ALU.mult).then_inc(s_keep, 1)
                        dve.wait_ge(s_keep, g * 4 + 2)
                        nc.vector.scalar_tensor_tensor(out=count[:, now], in0=dcol[:, now], scalar=m.lane[:], in1=keep[:, now],
                                                       op0=ALU.subtract, op1=ALU.mult).then_inc(s_keep, 1)
                        dve.wait_ge(s_keep, g * 4 + 3)
                        nc.vector.tensor_scalar(sidx[:, now], count[:, now], m.lane[:], None, ALU.add).then_inc(s_keep, 1)
                        dve.wait_ge(s_keep, g * 4 + 4)
                        nc.vector.tensor_copy(m.target[:, bass.ds(g * G, G)], sidx[:, now]).then_inc(s_sidx, 1)
                    else:
                        nc.vector.tensor_copy(sidx[:, now], m.target[:, bass.ds(g * G, G)]).then_inc(s_sidx, 1)
                    if not (isinstance(g, int) and g == NG - 1):
                        if not (isinstance(g, int) and g == 0):
                            dve.wait_ge(s_same, g * G)
                        give_dcol(g + 1, 1 - h)
                    if first_layer:
                        if not is_first(turn):
                            dve.wait_ge(s_counted, g - 1)
                        for j in range(G):
                            last = one_hot(nc, m, 1, g * G + j, low[:, h * G + j, :], high[:, h * G + j, :])
                        last.then_inc(s_hot, 1)
                    for j in range(G):
                        u = h * G + j
                        for k in range(K):
                            dve.wait_ge(s_row[k][u], turn * 16 + 16)
                        if K == 2:
                            nc.vector.tensor_tensor(rows[:, 0, u, :], rows[:, 0, u, :], rows[:, 1, u, :], ALU.add).then_inc(s_sum, 1)
                    if not one_before_last:
                        give_gidx(g + 2, h)
                each_group(dve, group)
                if first_layer:
                    dve.wait_ge(s_counted, NG + 1)
                    finish_degrees(nc, m, dve, 1, ps_hist, s_root)

            @block.scalar
            def _(act):
                def group(g, h, turn):
                    if K == 2:
                        for j in range(G):
                            u = h * G + j
                            act.wait_ge(s_sum, g * G + (j + 1))
                            nc.scalar.activation(rows[:, 0, u, :], rows[:, 0, u, :], ACT.Relu).then_inc(s_msg, 1)
                    act.wait_ge(s_merged, g + 1)
                    for j in range(G):
                        u = h * G + j
                        if not is_first(turn):
                            act.wait_ge(s_add[j % 2], g * 32 + (16 * (j // 2) - 48))
                        nc.scalar.copy(total[:, u, :], ps_m[:, h, j * P:(j + 1) * P]).then_inc(s_total, 1)
                each_group(act, group)
                if first_layer:
                    act.wait_ge(s_root, 1)
                    nc.scalar.activation(m.norm[:, 1, :], m.norm[:, 1, :], ACT.Sqrt).then_inc(s_root, 1)

            @block.tensor
            def _(pe):
                def spread_targets(g, h):
                    pe.wait_ge(s_dcol, g + 1)
                    if not (isinstance(g, int) and g < 2):
                        pe.wait_ge(s_same, g * G - G)
                    for j in range(G):
                        u = h * G + j
                        last = nc.tensor.transpose(ps_d[:, h, j * P:(j + 1) * P], dcol[:, u:u + 1].to_broadcast([P, P]), m.ident[:])
                    last.then_inc(s_drow, 1)

                spread_targets(0, 0)
                if first_layer:
                    nc.tensor.matmul(ps_hist[:, 0:COLS], m.zero_h[:, 0:P], m.zero_h[:], start=True, stop=False)

                def count(g, h):
                    pe.wait_ge(s_hot, g + 1)
                    for u in range(h * G, h * G + G):
                        last = nc.tensor.matmul(ps_hist[:, 0:COLS], low[:, u, :], high[:, u, :], start=False, stop=False)
                    last.then_inc(s_counted, 1)

                def group(g, h, turn):
                    if first_layer and not (isinstance(g, int) and g == 0):
                        count(g - 1, 1 - h)
                    if not (isinstance(g, int) and g == NG - 1):
                        spread_targets(g + 1, 1 - h)
                    if not is_first(turn):
                        pe.wait_ge(s_total, g * G - G)
                    for j in range(G):
                        u = h * G + j
                        pe.wait_ge(s_same, g * G + (j + 1))
                        if K == 2:
                            pe.wait_ge(s_msg, g * G + (j + 1))
                        else:
                            pe.wait_ge(s_row[0][u], turn * 16 + 16)
                        last = nc.tensor.matmul(ps_m[:, h, j * P:(j + 1) * P], same[:, u, :], rows[:, 0, u, :], start=True, stop=True)
                    last.then_inc(s_merged, 1)
                each_group(pe, group)
                if first_layer:
                    count(NG - 1, 1)
                    nc.tensor.matmul(ps_hist[:, 0:COLS], m.zero_h[:, 0:P], m.zero_h[:], start=False, stop=True).then_inc(s_counted, 1)


RING = 4


def pipelined(eng, steps):
    lags = [lag for _, lag in steps]
    first = -(-(RING + max(lags)) // RING)
    end = (NC - 1 + min(lags)) // RING

    def straight(steps_from, steps_to):
        for s in range(steps_from, steps_to):
            for body, lag in steps:
                c = s - lag
                if 0 <= c < NC:
                    body(c, c % RING, c // RING)

    straight(0, RING * first)
    with eng.Fori(first, end) as i:
        for b in range(RING):
            for body, lag in steps:
                body(i * RING + (b - lag), (b - lag) % RING, i + (b - lag) // RING)
    straight(RING * end, NC + max(lags))


def reused(c, ring):
    return not (isinstance(c, int) and c < ring)


def conv_stage(nc, m, x):
    with ExitStack() as ctx:
        sem = lambda n: m.semaphore(nc, n)
        sb = lambda n, ring=2: ctx.enter_context(nc.sbuf_tensor(m.tag + n, [P, ring, CH], F32))
        pb = lambda n: ctx.enter_context(nc.psum_tensor(m.tag + n, [P, 2, CH], F32))
        sum_a, sum_b, xin, g_t = (sb(n, RING) for n in ("sum_a", "sum_b", "xin", "g_t"))
        agg, agg_t, x_t, relu_t = (sb(n) for n in ("agg", "agg_t", "x_t", "relu_t"))
        ps_a, ps_x, ps_g, ps_r = (pb(n) for n in ("ps_a", "ps_x", "ps_g", "ps_r"))
        s_sa, s_sb, s_x, s_store = ([sem(f"{n}{b}") for b in range(RING)] for n in ("s_sa", "s_sb", "s_x", "s_store"))
        s_pair, s_agg, s_flip_a, s_flip_x, s_agg_t, s_x_t = (sem(n) for n in ("s_pair", "s_agg", "s_flip_a", "s_flip_x", "s_agg_t", "s_x_t"))
        s_conv, s_res, s_relu, s_g, s_stat, s_pad = (sem(n) for n in ("s_conv", "s_res", "s_relu", "s_g", "s_stat", "s_pad"))
        rows = lambda t: t.rearrange("p (j d) -> p j d", j=J)
        with nc.Block() as block:

            @block.sync
            def _(sp):
                sp.wait_ge(s_pad, 1)

                def load(c, b, turn):
                    if reused(c, RING):
                        sp.wait_ge(s_agg, c - (RING - 1))
                    sp.dma_start(sum_a[:, b, :], chunk(m.sums[0], c)).then_inc(s_sa[b], 16)
                    sp.dma_start(sum_b[:, b, :], chunk(m.sums[1], c)).then_inc(s_sb[b], 16)
                    if reused(c, RING):
                        sp.wait_ge(s_flip_x, c - (RING - 1))
                    sp.dma_start(xin[0:parts(c), b, :], chunk_rows(x, c)).then_inc(s_x[b], 16)

                def store(c, b, turn):
                    sp.wait_ge(s_g, c + 1)
                    sp.dma_start(m.table_g[bass.ds(c * P, P), :], g_t[:, b, :]).then_inc(s_store[b], 16)
                pipelined(sp, [(load, 0), (store, 5)])
                for b in range(RING):
                    sp.wait_ge(s_store[b], 16 * slot_uses(RING, b))

            @block.gpsimd
            def _(pool):
                def pair(c, b, turn):
                    pool.wait_ge(s_sa[b], turn * 16 + 16)
                    pool.wait_ge(s_sb[b], turn * 16 + 16)
                    nc.gpsimd.tensor_tensor(sum_a[:, b, :], sum_a[:, b, :], sum_b[:, b, :], ALU.add).then_inc(s_pair, 1)
                pipelined(pool, [(pair, 0)])

            @block.vector
            def _(dve):
                nc.vector.memset(xin[:], 0.0).then_inc(s_pad, 1)

                def scale(c, b, turn):
                    dve.wait_ge(s_pair, c + 1)
                    if reused(c, 2):
                        dve.wait_ge(s_flip_a, c - 1)
                    nc.vector.tensor_tensor(rows(agg[:, b % 2, :]), rows(sum_a[:, b, :]),
                                            m.norm[:, 1, bass.ds(c * J, J)].unsqueeze(2).to_broadcast([P, J, D]), ALU.mult).then_inc(s_agg, 1)

                def copy_x(c, b, turn):
                    dve.wait_ge(s_flip_x, c + 1)
                    if reused(c, 2):
                        dve.wait_ge(s_res, c - 1)
                    nc.vector.tensor_copy(x_t[:, b % 2, :], ps_x[:, b % 2, :]).then_inc(s_x_t, 1)

                def add(c, b, turn):
                    dve.wait_ge(s_res, c + 1)
                    dve.wait_ge(s_relu, c + 1)
                    if reused(c, RING):
                        dve.wait_ge(s_store[b], turn * 16)
                        dve.wait_ge(s_stat, c - (RING - 1))
                    nc.vector.scalar_tensor_tensor(out=g_t[:, b, :], in0=ps_r[:, b % 2, :], scalar=0.0, in1=relu_t[:, b % 2, :],
                                                   op0=ALU.max, op1=ALU.add).then_inc(s_g, 1)

                def stats(c, b, turn):
                    dve.wait_ge(s_g, c + 1)
                    if is_last(c):
                        for j in range(J):
                            last = nc.vector.bn_stats(m.stats[:, c + j, :], g_t[:, b, j * P:j * P + LAST])
                    else:
                        last = nc.vector.bn_stats(m.stats[:, bass.ds(c, 1), :].rearrange("p o s -> p (o s)"), g_t[:, b, :])
                    last.then_inc(s_stat, 1)
                pipelined(dve, [(scale, 0), (copy_x, 0), (add, 2), (stats, 2)])

            @block.scalar
            def _(act):
                def copy_agg(c, b, turn):
                    act.wait_ge(s_flip_a, c + 1)
                    if reused(c, 2):
                        act.wait_ge(s_conv, c - 1)
                    nc.scalar.copy(agg_t[:, b % 2, :], ps_a[:, b % 2, :]).then_inc(s_agg_t, 1)

                def relu(c, b, turn):
                    act.wait_ge(s_conv, c + 1)
                    if reused(c, 2):
                        act.wait_ge(s_g, c - 1)
                    nc.scalar.activation(relu_t[:, b % 2, :], ps_g[:, b % 2, :], ACT.Relu).then_inc(s_relu, 1)
                pipelined(act, [(copy_agg, 0), (relu, 1)])

            @block.tensor
            def _(pe):
                def flip(c, b, turn):
                    pe.wait_ge(s_x[b], turn * 16 + 16)
                    if reused(c, 2):
                        pe.wait_ge(s_x_t, c - 1)
                    for j in range(J):
                        last = nc.tensor.transpose(ps_x[:, b % 2, j * P:(j + 1) * P], xin[:, b, j * P:(j + 1) * P], m.ident[:])
                    last.then_inc(s_flip_x, 1)
                    pe.wait_ge(s_agg, c + 1)
                    if reused(c, 2):
                        pe.wait_ge(s_agg_t, c - 1)
                    for j in range(J):
                        last = nc.tensor.transpose(ps_a[:, b % 2, j * P:(j + 1) * P], agg[:, b % 2, j * P:(j + 1) * P], m.ident[:])
                    last.then_inc(s_flip_a, 1)

                def products(c, b, turn):
                    pe.wait_ge(s_x_t, c + 1)
                    if reused(c, 2):
                        pe.wait_ge(s_g, c - 1)
                    nc.tensor.matmul(ps_r[:, b % 2, :], m.wres[:], x_t[:, b % 2, :], start=True, stop=True).then_inc(s_res, 1)
                    pe.wait_ge(s_agg_t, c + 1)
                    if reused(c, 2):
                        pe.wait_ge(s_relu, c - 1)
                    nc.tensor.matmul(ps_g[:, b % 2, :], m.w0[:], agg_t[:, b % 2, :], start=True, stop=True).then_inc(s_conv, 1)
                pipelined(pe, [(flip, 0), (products, 1)])


def node_stage(nc, m, x, out, layer):
    conv, final = layer < 0, layer == L - 1
    nxt = layer + 1
    with ExitStack() as ctx:
        sem = lambda n: m.semaphore(nc, n)
        sems = lambda n: [sem(f"{n}{b}") for b in range(RING)]
        sb = lambda n, ring=2: ctx.enter_context(nc.sbuf_tensor(m.tag + n, [P, ring, CH], F32))
        small = lambda n, k: ctx.enter_context(nc.sbuf_tensor(m.tag + n, [P, 2, J, k], F32))
        in_a, in_b, in_c, extra, y, z, v, p_out, q_out, b_out, res = (sb(n, RING) for n in (
            "in_a", "in_b", "in_c", "extra", "y", "z", "v", "p_out", "q_out", "b_out", "res"))
        z_t, flat_t = sb("z_t"), sb("flat_t")
        st, mv, rstd, shift = small("st", 6), small("mv", 2), small("rstd", 1), small("shift", 1)
        st2, mv2, rstd2, shift2 = small("st2", 6), small("mv2", 2), small("rstd2", 1), small("shift2", 1)
        coef = ctx.enter_context(nc.sbuf_tensor(m.tag + "coef", [P, 8], F32))
        pbank = lambda n, k: ctx.enter_context(nc.psum_tensor(m.tag + n, [P, k, CH], F32))
        ps_in, ps_u, ps_t, ps_pb, ps_q = pbank("ps_in", 2), pbank("ps_u", 1), pbank("ps_t", 1), pbank("ps_pb", 2), pbank("ps_q", 2)
        s_a, s_b, s_c = sems("s_a"), sems("s_b"), sems("s_c")
        s_store = {k: sems(f"s_store_{k}") for k in "xpqb"}
        (s_pad, s_coef, s_lift, s_pair, s_flip, s_sum_t, s_upd, s_y, s_stat, s_aggr, s_rstd, s_norm, s_flip_z, s_z_t, s_proj,
         s_out_p, s_out_q, s_out_b, s_extra_m, s_extra, s_v, s_stat2, s_aggr2, s_rstd2, s_res, s_std, s_std2, s_go, s_proj_q, s_shift, s_shift2) = (sem(n) for n in (
             "s_pad", "s_coef", "s_lift", "s_pair", "s_flip", "s_sum_t", "s_upd", "s_y", "s_stat", "s_aggr", "s_rstd", "s_norm",
             "s_flip_z", "s_z_t", "s_proj", "s_out_p", "s_out_q", "s_out_b", "s_extra_m", "s_extra", "s_v", "s_stat2", "s_aggr2",
             "s_rstd2", "s_res", "s_std", "s_std2", "s_go", "s_proj_q", "s_shift", "s_shift2"))
        rows = lambda t: t.rearrange("p (j d) -> p j d", j=J)
        over_j = lambda t: t.unsqueeze(1).to_broadcast([P, J, D])
        with nc.Block() as block:

            @block.sync
            def _(sp):
                if conv:
                    sp.wait_ge(s_pad, 1)

                def load(c, b, turn):
                    again = reused(c, RING)
                    if conv:
                        if again:
                            sp.wait_ge(s_lift, c - (RING - 1))
                        sp.dma_start(in_a[:, b, :], m.table_g[bass.ds(c * P, P), :]).then_inc(s_a[b], 16)
                        if again:
                            sp.wait_ge(s_y, c - (RING - 1))
                        sp.dma_start(in_b[0:parts(c), b, :], chunk_rows(x, c)).then_inc(s_b[b], 16)
                    else:
                        if again:
                            sp.wait_ge(s_flip, c - (RING - 1))
                        sp.dma_start(in_a[:, b, :], chunk(m.sums[2 * nxt], c)).then_inc(s_a[b], 16)
                        sp.dma_start(in_b[:, b, :], chunk(m.sums[2 * nxt + 1], c)).then_inc(s_b[b], 16)
                        if again:
                            sp.wait_ge(s_y, c - (RING - 1))
                        sp.dma_start(in_c[:, b, :], chunk(m.table_b[layer], c)).then_inc(s_c[b], 16)

                def load_x1(c, b, turn):
                    if reused(c, RING):
                        sp.wait_ge(s_v, c - (RING - 1))
                    sp.dma_start(extra[:, b, :], chunk(m.table_x1, c)).then_inc(s_store["x"][b], 16)

                def store_x1(c, b, turn):
                    sp.wait_ge(s_norm, c * J + J)
                    sp.dma_start(chunk(m.table_x1, c), z[:, b, :]).then_inc(s_store["x"][b], 16)

                def store(c, b, turn):
                    if final:
                        sp.wait_ge(s_res, c * J + J)
                        sp.dma_start(chunk_rows(out, c), res[0:parts(c), b, :]).then_inc(s_store["b"][b], 16)
                        return
                    sp.wait_ge(s_out_p, c * 2 + 2)
                    sp.dma_start(chunk(m.table_p[nxt], c), p_out[:, b, :]).then_inc(s_store["p"][b], 16)
                    sp.wait_ge(s_out_b, c * 2 + 2)
                    sp.dma_start(chunk(m.table_b[nxt], c), b_out[:, b, :]).then_inc(s_store["b"][b], 16)
                pipelined(sp, [(load, 0)] + ([(load_x1, 5), (store, 11)] if final else
                                               [(store_x1, 5), (store, 8)] if conv else [(store, 8)]))
                for b in range(RING):
                    for k in ("b",) if final else ("x", "p", "b") if conv else ("p", "b"):
                        sp.wait_ge(s_store[k][b], 16 * slot_uses(RING, b))

            @block.gpsimd
            def _(pool):
                def pair(c, b, turn):
                    pool.wait_ge(s_a[b], turn * 16 + 16)
                    pool.wait_ge(s_b[b], turn * 16 + 16)
                    nc.gpsimd.tensor_tensor(in_a[:, b, :], in_a[:, b, :], in_b[:, b, :], ALU.add).then_inc(s_pair, 1)

                def add_extra(c, b, turn):
                    if final:
                        pool.wait_ge(s_store["x"][b], turn * 16 + 16)
                        nc.gpsimd.tensor_tensor(rows(extra[:, b, :]), rows(extra[:, b, :]), over_j(m.bout[:]), ALU.add).then_inc(s_extra, 1)
                        return
                    if reused(c, RING):
                        pool.wait_ge(s_out_b, c * 2 - 2 * (RING - 1))
                    nc.gpsimd.tensor_tensor(rows(extra[:, b, :]), over_j(m.ub2[:, nxt, :]),
                                            m.deg[:, 1, bass.ds(c * J, J)].unsqueeze(2).to_broadcast([P, J, D]), ALU.mult).then_inc(s_extra_m, 1)
                    pool.wait_ge(s_extra_m, c + 1)
                    nc.gpsimd.tensor_tensor(rows(extra[:, b, :]), rows(extra[:, b, :]), over_j(m.bu[:, nxt, :]), ALU.add).then_inc(s_extra, 1)

                pipelined(pool, ([] if conv else [(pair, 0)]) + [(add_extra, 5 if final else 4)])

            @block.scalar
            def _(act):
                if conv:
                    act.wait_ge(s_coef, 1)
                    nc.scalar.activation(coef[:, 2:3], coef[:, 1:2], ACT.Sqrt, bias=m.eps[:]).then_inc(s_coef, 1)
                    act.wait_ge(s_coef, 6)

                def head(c, b, turn):
                    again = reused(c, 2)
                    if conv:
                        act.wait_ge(s_a[b], turn * 16 + 16)
                        if again:
                            act.wait_ge(s_flip, c - 1)
                        nc.scalar.activation(flat_t[:, b % 2, :], in_a[:, b, :], ACT.Identity, scale=coef[:, 3:4],
                                             bias=coef[:, 5:6]).then_inc(s_lift, 1)
                    else:
                        act.wait_ge(s_flip, c + 1)
                        if again:
                            act.wait_ge(s_upd, c - 1)
                        nc.scalar.copy(flat_t[:, b % 2, :], ps_in[:, b % 2, :]).then_inc(s_sum_t, 1)

                def root(mv, rstd, s_aggr, s_std, s_done):
                    def body(c, b, turn):
                        act.wait_ge(s_aggr, c * J + J)
                        if reused(c, 2):
                            act.wait_ge(s_done, c * J - J)
                        nc.scalar.activation(rstd[:, b % 2, :, :], mv[:, b % 2, :, 1:2], ACT.Sqrt, bias=m.eps[:]).then_inc(s_std, 1)
                    return body

                def scale_rows(src, dst, rstd, shift, s_shift, s_done):
                    def body(c, b, turn):
                        act.wait_ge(s_shift, c + 1)
                        if reused(c, RING):
                            if dst is z:
                                act.wait_ge(s_flip_z, c - (RING - 1))
                            if dst is z and conv:
                                act.wait_ge(s_store["x"][b], turn * 16)
                            if dst is res:
                                act.wait_ge(s_store["b"][b], turn * 16)
                        for j in range(J):
                            nc.scalar.activation(dst[:, b, j * D:(j + 1) * D], src[:, b, j * D:(j + 1) * D], ACT.Identity,
                                                 scale=rstd[:, b % 2, j, :], bias=shift[:, b % 2, j, :]).then_inc(s_done, 1)
                    return body

                def store_q(c, b, turn):
                    act.wait_ge(s_out_q, c + 1)
                    act.dma_start(chunk(m.table_q[nxt], c), q_out[:, b, :]).then_inc(s_store["q"][b], 16)

                def copy_z(c, b, turn):
                    act.wait_ge(s_flip_z, c + 1)
                    if reused(c, 2):
                        act.wait_ge(s_proj_q if final else s_proj, c - 1 if final else c * 2 - 2)
                    nc.scalar.copy(z_t[:, b % 2, :], ps_t[:, 0, :]).then_inc(s_z_t, 1)

                def evacuate_q(c, b, turn):
                    act.wait_ge(s_proj_q, c + 1)
                    if reused(c, RING):
                        act.wait_ge(s_store["q"][b], turn * 16)
                    nc.scalar.copy(q_out[:, b, :], ps_q[:, b % 2, :]).then_inc(s_out_q, 1)
                norm_y, root_y = scale_rows(y, z, rstd, shift, s_shift, s_norm), root(mv, rstd, s_aggr, s_std, s_norm)
                norm_v, root_v = scale_rows(v, res, rstd2, shift2, s_shift2, s_res), root(mv2, rstd2, s_aggr2, s_std2, s_res)
                if final:
                    pipelined(act, [(head, 0), (norm_y, 4), (norm_v, 9), (root_y, 2), (root_v, 7), (copy_z, 5)])
                else:
                    pipelined(act, [(head, 0), (root_y, 2), (copy_z, 4), (norm_y, 3), (evacuate_q, 5), (store_q, 6)])
                    for b in range(2):
                        act.wait_ge(s_store["q"][b], 16 * slot_uses(RING, b))

            @block.tensor
            def _(pe):
                def flip(c, b, turn):
                    again = reused(c, 2)
                    pe.wait_ge(s_lift if conv else s_pair, c + 1)
                    if again:
                        pe.wait_ge(s_y if conv else s_sum_t, c - 1)
                    what = flat_t if conv else in_a
                    for j in range(J):
                        last = nc.tensor.transpose(ps_in[:, b % 2, j * P:(j + 1) * P], what[:, b % 2 if conv else b, j * P:(j + 1) * P], m.ident[:])
                    last.then_inc(s_flip, 1)

                def update(c, b, turn):
                    pe.wait_ge(s_sum_t, c + 1)
                    if not (isinstance(c, int) and c == 0):
                        pe.wait_ge(s_y, c)
                    for j in range(J):
                        last = nc.tensor.matmul(ps_u[:, 0, j * D:(j + 1) * D], flat_t[:, b % 2, j * P:(j + 1) * P], m.uw[:, layer, :],
                                                start=True, stop=True)
                    last.then_inc(s_upd, 1)

                def flip_z(c, b, turn):
                    pe.wait_ge(s_norm, c * J + J)
                    if not (isinstance(c, int) and c == 0):
                        pe.wait_ge(s_z_t, c)
                    for j in range(J):
                        last = nc.tensor.transpose(ps_t[:, 0, j * P:(j + 1) * P], z[:, b, j * P:(j + 1) * P], m.ident[:])
                    last.then_inc(s_flip_z, 1)

                def project(c, b, turn):
                    pe.wait_ge(s_z_t, c + 1)
                    if reused(c, 2):
                        pe.wait_ge(s_v if final else s_out_q, c - 1)
                    for j in range(J):
                        w = m.wout[:] if final else m.wproj[:, nxt, D:2 * D]
                        last = nc.tensor.matmul(ps_q[:, b % 2, j * D:(j + 1) * D], z_t[:, b % 2, j * P:(j + 1) * P], w, start=True, stop=True)
                    last.then_inc(s_proj_q, 1)
                    if final:
                        return
                    for h in range(2):
                        if not (isinstance(c, int) and c == 0):
                            pe.wait_ge(s_out_b, c * 2 + (h - 1))
                        for k in range(2):
                            j = 2 * h + k
                            last = nc.tensor.matmul(ps_pb[:, h, k * 2 * D:(k + 1) * 2 * D], z_t[:, b % 2, j * P:(j + 1) * P],
                                                    m.wproj[:, nxt, :].rearrange("p (k d) -> p k d", k=3)[:, 0:3:2, :],
                                                    start=True, stop=True)
                        last.then_inc(s_proj, 1)
                pipelined(pe, [(flip, 1 if conv else 0), (flip_z, 5 if final else 4)] + ([] if conv else [(update, 1)]) + [(project, 6 if final else 5)])

            @block.vector
            def _(dve):
                if conv:
                    links = [0]

                    def link(ins):
                        links[0] += 1
                        ins.then_inc(s_coef, 1)
                        dve.wait_ge(s_coef, links[0])
                    nc.vector.memset(in_b[:], 0.0).then_inc(s_pad, 1)
                    link(nc.vector.bn_aggr(coef[:, 0:2], m.stats[:].rearrange("p c s -> p (c s)")))
                    dve.wait_ge(s_coef, 2)
                    links[0] += 1
                    link(nc.vector.reciprocal(coef[:, 2:3], coef[:, 2:3]))
                    link(nc.vector.tensor_tensor(coef[:, 3:4], coef[:, 2:3], m.bn[:, 0:1], ALU.mult))
                    link(nc.vector.tensor_tensor(coef[:, 4:5], coef[:, 0:1], coef[:, 3:4], ALU.mult))
                    link(nc.vector.tensor_tensor(coef[:, 5:6], m.bn[:, 1:2], coef[:, 4:5], ALU.subtract))

                def make_y(c, b, turn):
                    if conv:
                        dve.wait_ge(s_flip, c + 1)
                        dve.wait_ge(s_b[b], turn * 16 + 16)
                    else:
                        dve.wait_ge(s_upd, c + 1)
                        dve.wait_ge(s_c[b], turn * 16 + 16)
                    if reused(c, RING):
                        dve.wait_ge(s_norm, c * J - J * (RING - 1))
                    nc.vector.tensor_tensor(y[:, b, :], ps_in[:, b % 2, :] if conv else ps_u[:, 0, :],
                                            in_b[:, b, :] if conv else in_c[:, b, :], ALU.add).then_inc(s_y, 1)

                def statistics(src, st, ready, s_stat, c, b):
                    dve.wait_ge(ready, c + 1)
                    for j in range(J):
                        nc.vector.bn_stats(st[:, b % 2, j, :], src[:, b, j * D:(j + 1) * D]).then_inc(s_stat, 1)

                def moments(st, mv, s_stat, s_aggr, c, b):
                    dve.wait_ge(s_stat, c * J + J)
                    dve.sem_inc(s_go, 1)
                    for j in range(J):
                        nc.vector.bn_aggr(mv[:, b % 2, j, :], st[:, b % 2, j, :]).then_inc(s_aggr, 1)

                def invert(rstd, s_std, s_rstd, c, b):
                    dve.wait_ge(s_std, c + 1)
                    nc.vector.reciprocal(rstd[:, b % 2, :, :], rstd[:, b % 2, :, :]).then_inc(s_rstd, 1)

                def offset(mv, rstd, shift, s_rstd, s_shift, s_done, c, b):
                    dve.wait_ge(s_rstd, c + 1)
                    if reused(c, 2):
                        dve.wait_ge(s_done, c * J - J)
                    nc.vector.scalar_tensor_tensor(out=shift[:, b % 2, :, :], in0=mv[:, b % 2, :, 0:1], scalar=-1.0, in1=rstd[:, b % 2, :, :],
                                                   op0=ALU.mult, op1=ALU.mult).then_inc(s_shift, 1)

                stats_y = lambda c, b, turn: statistics(y, st, s_y, s_stat, c, b)
                moments_y = lambda c, b, turn: moments(st, mv, s_stat, s_aggr, c, b)
                invert_y = lambda c, b, turn: invert(rstd, s_std, s_rstd, c, b)
                offset_y = lambda c, b, turn: offset(mv, rstd, shift, s_rstd, s_shift, s_norm, c, b)
                stats_v = lambda c, b, turn: statistics(v, st2, s_v, s_stat2, c, b)
                moments_v = lambda c, b, turn: moments(st2, mv2, s_stat2, s_aggr2, c, b)
                invert_v = lambda c, b, turn: invert(rstd2, s_std2, s_rstd2, c, b)
                offset_v = lambda c, b, turn: offset(mv2, rstd2, shift2, s_rstd2, s_shift2, s_res, c, b)

                def evacuate(c, b, turn):
                    for h in range(2):
                        dve.wait_ge(s_proj, c * 2 + (h + 1))
                        if h == 0:
                            if reused(c, RING):
                                dve.wait_ge(s_store["p"][b], turn * 16)
                                dve.wait_ge(s_store["b"][b], turn * 16)
                            dve.wait_ge(s_extra, c + 1)
                        two = slice(2 * h, 2 * h + 2)
                        both = ps_pb[:, h, :].rearrange("p (k t d) -> p k t d", k=2, t=2)
                        nc.vector.tensor_tensor(rows(p_out[:, b, :])[:, two, :], both[:, :, 0, :],
                                                m.bp[:, nxt, :].unsqueeze(1).to_broadcast([P, 2, D]), ALU.add).then_inc(s_out_p, 1)
                        nc.vector.tensor_tensor(rows(b_out[:, b, :])[:, two, :], both[:, :, 1, :],
                                                rows(extra[:, b, :])[:, two, :], ALU.add).then_inc(s_out_b, 1)

                def make_v(c, b, turn):
                    dve.wait_ge(s_proj_q, c + 1)
                    dve.wait_ge(s_extra, c + 1)
                    if reused(c, RING):
                        dve.wait_ge(s_res, c * J - J * (RING - 1))
                    nc.vector.tensor_tensor(v[:, b, :], ps_q[:, b % 2, :], extra[:, b, :], ALU.add).then_inc(s_v, 1)

                if final:
                    pipelined(dve, [(invert_y, 3), (invert_v, 8), (make_y, 1), (make_v, 6), (offset_y, 3), (offset_v, 8),
                                    (stats_y, 1), (stats_v, 6), (moments_y, 1), (moments_v, 6)])
                else:
                    pipelined(dve, [(make_y, 1), (stats_y, 1), (moments_y, 1), (evacuate, 5), (invert_y, 2), (offset_y, 2)])


def build(nc, a, out):
    m = Mem()
    table = lambda n, r, w: nc.dram_tensor(n, [r, w], F32, kind="Internal").ap()
    m.table_h, m.table_x1 = table("table_h", NPAD, D), table("table_x1", NPAD, D)
    m.table_g = table("table_g", NC * P, CH)
    m.table_p, m.table_q, m.table_b = ([table(f"table_{k}{l}", NPAD, D) for l in range(L)] for k in "pqb")
    m.sums = [table(f"sums{k}", AGG, D) for k in range(2 * (L + 1))]
    with ExitStack() as ctx:
        sb = lambda n, s, d=F32: ctx.enter_context(nc.sbuf_tensor(n, s, d))
        m.edge, m.gather = sb("edge", [P, 2, TP], I32), sb("gather", [P, 2, TP], I32)
        m.target, m.dstf = sb("target", [P, TP], I32), sb("dstf", [P, TP])
        m.deg, m.norm = sb("deg", [P, 2, COLS]), sb("norm", [P, 2, COLS])
        m.ident, m.upper, m.lane, m.eps = sb("ident", [P, P]), sb("upper", [P, P]), sb("lane", [P, 1]), sb("eps", [P, 1])
        m.w0, m.wres, m.wproj, m.wout = sb("w0", [P, D]), sb("wres", [P, D]), sb("wproj", [P, L, 3 * D]), sb("wout", [P, D])
        m.uw, m.ub2 = sb("uw", [P, L, D]), sb("ub2", [P, L, D])
        m.bp, m.bq, m.bu, m.bout, m.bn = sb("bp", [P, L, D]), sb("bq", [P, L, D]), sb("bu", [P, L, D]), sb("bout", [P, D]), sb("bn", [P, 2])
        m.iota, m.zero_h, m.zeros = sb("iota", [P, COLS], F16), sb("zero_h", [P, COLS], F16), sb("zeros", [P, 2048])
        m.bins = sb("bins", [P, 4, TP])
        m.stats = sb("stats", [P, NC - 1 + J, 6])
        def stage(name, make, *args):
            m.tag, m.sems = name + "_", []
            make(nc, m, *args)
            nc.clear_and_free_semaphores(m.sems)
            nc.all_engine_barrier()
        stage("setup", setup_stage, a)
        stage("weights", weight_stage, a)
        stage("scale", scale_stage, a["x"])
        stage("edges", edge_stage, [m.table_h], m.sums[0:2], m.sums[2:], True)
        stage("conv", conv_stage, a["x"])
        stage("nodes", node_stage, a["x"], out, -1)
        for l in range(L):
            stage(f"edges{l}", edge_stage, [m.table_p[l], m.table_q[l]], m.sums[2 * l + 2:2 * l + 4], None, False)
            stage(f"nodes{l}", node_stage, a["x"], out, l)


def kernel(**inputs):
    import numpy as np
    import concourse.bacc as bacc
    from concourse.bass_utils import run_bass_kernel_spmd as run
    nc = bacc.Bacc("TRN2", target_bir_lowering=False, num_devices=1)
    arrays, a = {}, {}
    for name, value in inputs.items():
        value = np.ascontiguousarray(value)
        arrays[f"in_{name}"] = value
        a[name] = nc.dram_tensor(f"in_{name}", value.shape, mybir.dt.from_np(value.dtype), kind="ExternalInput").ap()
    out = nc.dram_tensor("out_0", (N, D), F32, kind="ExternalOutput").ap()
    build(nc, a, out)
    return run(nc, [arrays], core_ids=[0]).results[0]["out_0"]
```
